# Optimizing a Trainium2 kernel written in Bass

```python
import numpy as np
import jax
import jax.numpy as jnp

def _softmax(x, axis=-1):
    return jax.nn.softmax(x, axis=axis)

def _gelu(x):
    return jax.nn.gelu(x, approximate=True)

def _silu(x):
    return jax.nn.silu(x)

def _sigmoid(x):
    return jax.nn.sigmoid(x)

def _layernorm(x, axis=-1, eps=1e-05):
    m = jnp.mean(x, axis=axis, keepdims=True)
    v = jnp.var(x, axis=axis, keepdims=True)
    return (x - m) / jnp.sqrt(v + eps)

def _scatter_add(tgt, idx, src, axis=0):
    return tgt.at[idx].add(src)

def _segment_sum(src, seg, n):
    return jax.ops.segment_sum(src, seg, n)
kernel_name = 'mk_perceiver_d1_seqx_r4_8ad4e3'

def setup_inputs(seed: int=0):
    np.random.seed(seed)
    _w = jnp.asarray

    def _rec_inputs():
        import jax
        import jax.numpy as jnp
        _rk = jax.random.key(seed)
        x = -0.0002928 + 1 * jax.random.normal(jax.random.fold_in(_rk, 1), (16, 64, 512), jnp.float32)
        _lenS = 64 - jax.random.randint(jax.random.fold_in(_rk, 7), (16,), 0, max(1, 64 // 4) + 1, jnp.int32)
        _lenS2 = 1024 - jax.random.randint(jax.random.fold_in(_rk, 8), (16,), 0, max(1, 1024 // 4) + 1, jnp.int32)
        _ctx_512P = jax.random.normal(jax.random.fold_in(_rk, 11), (16, 16, 128), jnp.float32)
        _ctx_512c = jax.random.dirichlet(jax.random.fold_in(_rk, 511), 0.3 * jnp.ones((16,), jnp.float32), (16, 1024))
        _ctx_512t = jnp.einsum('bsk,bkd->bsd', _ctx_512c, _ctx_512P)
        _ctx_512t = _ctx_512t * jax.lax.rsqrt(jnp.mean(jnp.square(_ctx_512t)) + 1e-12) * 0.953939
        ctx_512 = 0.000227908 + 0.99994 * (_ctx_512t + 0.3 * jax.random.normal(jax.random.fold_in(_rk, 611), (16, 1024, 128), jnp.float32))
        return (x, ctx_512)
    x, ctx_512 = _rec_inputs()

    def _L0_xattn_setup():
        import jax, jax.numpy as jnp
        import numpy as np
        B, S, L = (2, 256, 256)
        DIM_Q, H, K, D_C, D_CQ, R = (512, 16, 128, 128, 384, 64)

        def _rope_tables(seq_len, dim, dtype):
            inv_freq = 1.0 / 10000.0 ** (jnp.arange(0, dim, 2, dtype=dtype) / dim)
            t = jnp.arange(seq_len, dtype=dtype)
            freqs = t[:, None] * inv_freq[None, :]
            sin = jnp.repeat(jnp.sin(freqs), 2, axis=-1)
            cos = jnp.repeat(jnp.cos(freqs), 2, axis=-1)
            return (sin, cos)

        def _rotate_half(x):
            h = x.shape[-1] // 2
            return jnp.concatenate([-x[..., h:], x[..., :h]], axis=-1)
        key = jax.random.key(seed)
        ks = jax.random.split(key, 8)
        s_in = 1.0 / np.sqrt(DIM_Q)
        s_k = 1.0 / np.sqrt(K)
        s_cq = 1.0 / np.sqrt(D_CQ)
        s_c = 1.0 / np.sqrt(D_C)
        return {'hidden_q': jax.random.normal(ks[0], (B, S, DIM_Q), jnp.float32), 'kv_c': jax.random.normal(ks[1], (B, L, D_C), jnp.float32), 'Wq': jax.random.normal(ks[2], (H * K, DIM_Q), jnp.float32) * s_in, 'w_kc_q': jax.random.normal(ks[3], (H, K, D_CQ), jnp.float32) * s_k, 'w_kc_kv': jax.random.normal(ks[4], (H, K, D_C), jnp.float32) * s_k, 'W_qr': jax.random.normal(ks[5], (H, D_CQ, R), jnp.float32) * s_cq / np.sqrt(R), 'W_kr': jax.random.normal(ks[6], (H, D_C, R), jnp.float32) * s_c, 'Wo': jax.random.normal(ks[7], (DIM_Q, H * K), jnp.float32) * s_k}
    _L0_xattn_all = _L0_xattn_setup()
    _L0_xattn_in = {k: v for k, v in _L0_xattn_all.items() if k in ('Wq', 'w_kc_q', 'w_kc_kv', 'W_qr', 'W_kr', 'Wo')}
    del _L0_xattn_all

    def _L0_attn_setup():
        import jax, jax.numpy as jnp
        import numpy as np
        HIDDEN = 512
        HQ = 32
        HKV = 4
        D = 64
        THETA = 10000.0
        SEQ = 512

        def _rope(x, pos):
            d = x.shape[-1]
            inv = 1.0 / THETA ** (jnp.arange(0, d, 2, dtype=jnp.float32) / d)
            ang = pos[:, None] * inv
            cos = jnp.cos(ang)[None, :, None, :]
            sin = jnp.sin(ang)[None, :, None, :]
            x1, x2 = jnp.split(x, 2, axis=-1)
            return jnp.concatenate([x1 * cos - x2 * sin, x2 * cos + x1 * sin], axis=-1)
        key = jax.random.key(seed)
        k1, k2, k3 = jax.random.split(key, 3)
        hidden_states = jax.random.normal(k1, (1, SEQ, HIDDEN), jnp.float32)
        w_qkv = jax.random.normal(k2, ((HQ + 2 * HKV) * D, HIDDEN), jnp.float32) * 0.02
        w_o = jax.random.normal(k3, (HIDDEN, HQ * D), jnp.float32) * 0.02
        return {'hidden_states': hidden_states, 'w_qkv': w_qkv, 'w_o': w_o}
    _L0_attn_all = _L0_attn_setup()
    _L0_attn_in = {k: v for k, v in _L0_attn_all.items() if k in ('w_qkv', 'w_o')}
    del _L0_attn_all

    def _L0_ffn_setup():
        import jax, jax.numpy as jnp
        import numpy as np
        NUM_EXPERTS = 16
        TOP_K = 4
        N_GROUP = 4
        TOPK_GROUP = 2
        SCALING = 2.5

        def _route(x, gate_weight, expert_bias):
            logits = x @ gate_weight.T
            scores = jax.nn.sigmoid(logits)
            biased = scores + expert_bias[None, :]
            T = x.shape[0]
            gsz = NUM_EXPERTS // N_GROUP
            grp = biased.reshape(T, N_GROUP, gsz)
            top2, _ = jax.lax.top_k(grp, 2)
            group_scores = top2.sum(-1)
            _, gidx = jax.lax.top_k(group_scores, TOPK_GROUP)
            gmask = jax.nn.one_hot(gidx, N_GROUP, dtype=scores.dtype).sum(1)
            emask = jnp.repeat(gmask, gsz, axis=1)
            masked = jnp.where(emask > 0, biased, -jnp.inf)
            _, sel = jax.lax.top_k(masked, TOP_K)
            w = jnp.take_along_axis(scores, sel, axis=1)
            w = w / (w.sum(-1, keepdims=True) + 1e-20)
            return (w * SCALING, sel)

        def _moe(x, w, sel, gate_proj, up_proj, down_proj):
            cw = (jax.nn.one_hot(sel, NUM_EXPERTS, dtype=x.dtype) * w[..., None]).sum(1)

            def body(acc, inp):
                g, u, d, we = inp
                y = jax.nn.silu(x @ g.T) * (x @ u.T) @ d.T
                return (acc + we[:, None] * y, None)
            out, _ = jax.lax.scan(body, jnp.zeros_like(x), (gate_proj, up_proj, down_proj, cw.T))
            return out
        key = jax.random.key(seed)
        ks = jax.random.split(key, 9)
        B, S, H, I = (2, 256, 512, 256)
        w = lambda k, shape: jax.random.normal(k, shape, jnp.float32) * 0.02
        return {'hidden_states': jax.random.normal(ks[0], (B, S, H), jnp.float32), 'gate_weight': w(ks[1], (NUM_EXPERTS, H)), 'expert_bias': jnp.zeros((NUM_EXPERTS,), jnp.float32), 'gate_proj': w(ks[2], (NUM_EXPERTS, I, H)), 'up_proj': w(ks[3], (NUM_EXPERTS, I, H)), 'down_proj': w(ks[4], (NUM_EXPERTS, H, I)), 'shared_gate': w(ks[5], (I, H)), 'shared_up': w(ks[6], (I, H)), 'shared_down': w(ks[7], (H, I))}
    _L0_ffn_all = _L0_ffn_setup()
    _L0_ffn_in = {k: v for k, v in _L0_ffn_all.items() if k in ('gate_weight', 'expert_bias', 'gate_proj', 'up_proj', 'down_proj', 'shared_gate', 'shared_up', 'shared_down')}
    del _L0_ffn_all
    return {'x': x, 'ctx_512': ctx_512, 'L0_xattn_Wq': _L0_xattn_in['Wq'], 'L0_xattn_w_kc_q': _L0_xattn_in['w_kc_q'], 'L0_xattn_w_kc_kv': _L0_xattn_in['w_kc_kv'], 'L0_xattn_W_qr': _L0_xattn_in['W_qr'], 'L0_xattn_W_kr': _L0_xattn_in['W_kr'], 'L0_xattn_Wo': _L0_xattn_in['Wo'], 'L0_attn_w_qkv': _L0_attn_in['w_qkv'], 'L0_attn_w_o': _L0_attn_in['w_o'], 'L0_ffn_gate_weight': _L0_ffn_in['gate_weight'], 'L0_ffn_expert_bias': _L0_ffn_in['expert_bias'], 'L0_ffn_gate_proj': _L0_ffn_in['gate_proj'], 'L0_ffn_up_proj': _L0_ffn_in['up_proj'], 'L0_ffn_down_proj': _L0_ffn_in['down_proj'], 'L0_ffn_shared_gate': _L0_ffn_in['shared_gate'], 'L0_ffn_shared_up': _L0_ffn_in['shared_up'], 'L0_ffn_shared_down': _L0_ffn_in['shared_down']}

def reference(x, ctx_512, L0_xattn_Wq, L0_xattn_w_kc_q, L0_xattn_w_kc_kv, L0_xattn_W_qr, L0_xattn_W_kr, L0_xattn_Wo, L0_attn_w_qkv, L0_attn_w_o, L0_ffn_gate_weight, L0_ffn_expert_bias, L0_ffn_gate_proj, L0_ffn_up_proj, L0_ffn_down_proj, L0_ffn_shared_gate, L0_ffn_shared_up, L0_ffn_shared_down):
    import jax
    import jax.numpy as jnp

    def _L0_xattn_ref(hidden_q, kv_c, Wq, w_kc_q, w_kc_kv, W_qr, W_kr, Wo):
        import jax, jax.numpy as jnp
        import numpy as np
        B, S, L = (2, 256, 256)
        DIM_Q, H, K, D_C, D_CQ, R = (512, 16, 128, 128, 384, 64)

        def _rope_tables(seq_len, dim, dtype):
            inv_freq = 1.0 / 10000.0 ** (jnp.arange(0, dim, 2, dtype=dtype) / dim)
            t = jnp.arange(seq_len, dtype=dtype)
            freqs = t[:, None] * inv_freq[None, :]
            sin = jnp.repeat(jnp.sin(freqs), 2, axis=-1)
            cos = jnp.repeat(jnp.cos(freqs), 2, axis=-1)
            return (sin, cos)

        def _rotate_half(x):
            h = x.shape[-1] // 2
            return jnp.concatenate([-x[..., h:], x[..., :h]], axis=-1)
        b, s, _ = hidden_q.shape
        l = kv_c.shape[1]
        q_hk = (hidden_q @ Wq.T).reshape(b, s, H, K)
        q_big = jnp.einsum('bshk,hkq->bshq', q_hk, w_kc_q)
        sin, cos = _rope_tables(l, D_C, kv_c.dtype)
        kv_rope = kv_c * cos[None] + _rotate_half(kv_c) * sin[None]
        q_r = jnp.einsum('bshq,hqr->bhsr', q_big, W_qr)
        k_r = jnp.einsum('bld,hdr->bhlr', kv_rope, W_kr)
        scores = jnp.einsum('bhsr,bhlr->bhsl', q_r, k_r)
        attn = jax.nn.softmax(scores, axis=-1)
        ctx_c = jnp.einsum('bhsl,bld->bhsd', attn, kv_rope)
        ctx_lat = jnp.einsum('bhsd,hkd->bshk', ctx_c, w_kc_kv)
        out = ctx_lat.reshape(b, s, H * K) @ Wo.T
        return out

    def _L0_attn_ref(hidden_states, w_qkv, w_o):
        import jax, jax.numpy as jnp
        import numpy as np
        HIDDEN = 512
        HQ = 32
        HKV = 4
        D = 64
        THETA = 10000.0
        SEQ = 512

        def _rope(x, pos):
            d = x.shape[-1]
            inv = 1.0 / THETA ** (jnp.arange(0, d, 2, dtype=jnp.float32) / d)
            ang = pos[:, None] * inv
            cos = jnp.cos(ang)[None, :, None, :]
            sin = jnp.sin(ang)[None, :, None, :]
            x1, x2 = jnp.split(x, 2, axis=-1)
            return jnp.concatenate([x1 * cos - x2 * sin, x2 * cos + x1 * sin], axis=-1)
        b, s, _ = hidden_states.shape
        qkv = jnp.einsum('bsh,oh->bso', hidden_states, w_qkv).reshape(b, s, HQ + 2 * HKV, D)
        q = qkv[:, :, :HQ]
        k = qkv[:, :, HQ:HQ + HKV]
        v = qkv[:, :, HQ + HKV:]
        pos = jnp.arange(s, dtype=jnp.float32)
        q = _rope(q, pos)
        k = _rope(k, pos)
        rep = HQ // HKV
        k = jnp.repeat(k, rep, axis=2)
        v = jnp.repeat(v, rep, axis=2)
        scores = jnp.einsum('bqhd,bkhd->bhqk', q, k) * D ** (-0.5)
        causal = jnp.tril(jnp.ones((s, s), dtype=bool))
        scores = jnp.where(causal[None, None], scores, jnp.finfo(scores.dtype).min)
        attn = jax.nn.softmax(scores, axis=-1)
        out = jnp.einsum('bhqk,bkhd->bqhd', attn, v).reshape(b, s, HQ * D)
        return jnp.einsum('bso,ho->bsh', out, w_o)

    def _L0_ffn_ref(hidden_states, gate_weight, expert_bias, gate_proj, up_proj, down_proj, shared_gate, shared_up, shared_down):
        import jax, jax.numpy as jnp
        import numpy as np
        NUM_EXPERTS = 16
        TOP_K = 4
        N_GROUP = 4
        TOPK_GROUP = 2
        SCALING = 2.5

        def _route(x, gate_weight, expert_bias):
            logits = x @ gate_weight.T
            scores = jax.nn.sigmoid(logits)
            biased = scores + expert_bias[None, :]
            T = x.shape[0]
            gsz = NUM_EXPERTS // N_GROUP
            grp = biased.reshape(T, N_GROUP, gsz)
            top2, _ = jax.lax.top_k(grp, 2)
            group_scores = top2.sum(-1)
            _, gidx = jax.lax.top_k(group_scores, TOPK_GROUP)
            gmask = jax.nn.one_hot(gidx, N_GROUP, dtype=scores.dtype).sum(1)
            emask = jnp.repeat(gmask, gsz, axis=1)
            masked = jnp.where(emask > 0, biased, -jnp.inf)
            _, sel = jax.lax.top_k(masked, TOP_K)
            w = jnp.take_along_axis(scores, sel, axis=1)
            w = w / (w.sum(-1, keepdims=True) + 1e-20)
            return (w * SCALING, sel)

        def _moe(x, w, sel, gate_proj, up_proj, down_proj):
            cw = (jax.nn.one_hot(sel, NUM_EXPERTS, dtype=x.dtype) * w[..., None]).sum(1)

            def body(acc, inp):
                g, u, d, we = inp
                y = jax.nn.silu(x @ g.T) * (x @ u.T) @ d.T
                return (acc + we[:, None] * y, None)
            out, _ = jax.lax.scan(body, jnp.zeros_like(x), (gate_proj, up_proj, down_proj, cw.T))
            return out
        B, S, H = hidden_states.shape
        x = hidden_states.reshape(-1, H)
        w, sel = _route(x, gate_weight, expert_bias)
        out = _moe(x, w, sel, gate_proj, up_proj, down_proj)
        shared = jax.nn.silu(x @ shared_gate.T) * (x @ shared_up.T) @ shared_down.T
        return (out + shared).reshape(B, S, H)
    x = x + _L0_xattn_ref(_layernorm(x, axis=-1), ctx_512, L0_xattn_Wq, L0_xattn_w_kc_q, L0_xattn_w_kc_kv, L0_xattn_W_qr, L0_xattn_W_kr, L0_xattn_Wo)
    x = x + _L0_attn_ref(_layernorm(x, axis=-1), L0_attn_w_qkv, L0_attn_w_o)
    x = x + _L0_ffn_ref(_layernorm(x, axis=-1), L0_ffn_gate_weight, L0_ffn_expert_bias, L0_ffn_gate_proj, L0_ffn_up_proj, L0_ffn_down_proj, L0_ffn_shared_gate, L0_ffn_shared_up, L0_ffn_shared_down)
    return x

_drawn_inputs = setup_inputs


def setup_inputs(seed=0):
    import zlib

    import numpy as np

    out = dict(_drawn_inputs(seed))
    spreads = {'L0_ffn_expert_bias': (0.0, 0.328)}
    factors = {'L0_ffn_gate_weight': 3.155,
     'L0_ffn_shared_gate': 2.823,
     'L0_ffn_shared_up': 2.77,
     'L0_ffn_shared_down': 2.761}
    for name, (base, spread) in spreads.items():
        noise = np.random.default_rng([zlib.crc32(name.encode()), seed]).standard_normal(out[name].shape)
        drawn = base * np.exp(spread * noise) if base else spread * noise
        out[name] = jnp.asarray(drawn.astype(out[name].dtype))
    for name, factor in factors.items():
        out[name] = (out[name] * factor).astype(out[name].dtype)
    return out
```

```python
from contextlib import ExitStack

import numpy as np

import concourse.bass as bass
from concourse import mybir

F32 = mybir.dt.float32
F32R = mybir.dt.float32r
ALU = mybir.AluOpType
ACT = mybir.ActivationFunctionType
AX = mybir.AxisListType

P = 128
B, S, D = 16, 64, 512
T = B * S
NT = T // P
KC = D // P
EPS = 1e-5
BANK = 512

L, DC, H, R, CQ = 1024, 128, 16, 64, 384
NP = H // 2
QT = CQ // P
LT = L // P
W_KQ, W_QR, W_Q = 2 * QT * P, 2 * QT * R, 2 * D
W_KR, W_KV, W_O = P, 2 * DC, 2 * D
W_A = W_KQ + W_QR + W_Q
W_B = W_KR + W_KV + W_O

HQ, HKV, DH = 32, 4, 64
REP = HQ // HKV

NE, TOPK, NG, TOPG, I = 16, 4, 4, 2, 256
GS = NE // NG
SCALING = 2.5
NIT = I // P


def mm3(pe, out, lhs, rhs, start, stop):
    pe.matmul(out, lhs[0], rhs[0], start=start, stop=False, skip_group_check=True)
    pe.matmul(out, lhs[0], rhs[1], start=False, stop=False, skip_group_check=True)
    return pe.matmul(out, lhs[1], rhs[0], start=False, stop=stop, skip_group_check=True)


class Pair:

    def __init__(self, ctx, nc, name, shape):
        self.hi = ctx.enter_context(nc.sbuf_tensor(name + "_hi", shape, F32R))
        self.lo = ctx.enter_context(nc.sbuf_tensor(name + "_lo", shape, F32R))

    def at(self, *idx):
        return self.hi[idx], self.lo[idx]


def f32(ap):
    return ap.bitcast(F32)


ALL = slice(None)


def build_queries(nc, ctx, sem, x_d, w_pairs, qe_d, keep):
    ident, F, h1T, eps_pow = keep["ident"], keep["F"], keep["h1T"], keep["eps_pow"]

    def sb(name, shape, dt=F32):
        return ctx.enter_context(nc.sbuf_tensor(name, shape, dt))

    XP = 4
    T_AT, C_AT = 4, 6
    raw = [sb(f"wraw{j}", [P, W_A + W_B]) for j in range(2)]
    WB = [Pair(ctx, nc, f"wb{j}", [P, W_B]) for j in range(2)]
    TW = sb("tw", [P, 2, R])
    C = Pair(ctx, nc, "cfold", [P, KC, P])
    Q = Pair(ctx, nc, "qr", [P, T])
    stage = sb("stage", [P, 2, T * 2])
    x_all = stage[:, :, :].rearrange("p a (b c) -> p (a b) c", c=D)
    stage_o = stage[:, :, :].rearrange("p a (b x) -> p a b x", b=B)
    stage_w = stage[:, :, :].bitcast(F32R).rearrange("p a (b j s) -> p a b j s", b=B, j=2)
    st = sb("st1", [P, NT, 6])
    mv = sb("mv1", [P, NT, 2])
    var = sb("var1", [P, NT])
    rstd = sb("rstd1", [P, NT])
    h = [sb(f"h1_{j}", [P, D]) for j in range(2)]

    psQ = ctx.enter_context(nc.psum_tensor("psQ", [P, 2, BANK], F32))
    psE = ctx.enter_context(nc.psum_tensor("psE", [P, 2, BANK], F32))
    psF = ctx.enter_context(nc.psum_tensor("psF", [P, 2, BANK], F32))
    psT = ctx.enter_context(nc.psum_tensor("psT", [P, BANK], F32))
    psC = ctx.enter_context(nc.psum_tensor("psC", [P, BANK], F32))

    x_in = [sem(f"x_in{a}") for a in range(XP)]
    w_in = [sem(f"w_in{j}") for j in range(2)]
    const_set, ln1, rstd1, h1_made = sem("const_set"), sem("ln1"), sem("rstd1"), sem("h1_made")
    h1_turned, h1_hi, h1_lo = sem("h1_turned"), sem("h1_hi"), sem("h1_lo")
    wB_hi, wB_ready = sem("wB_hi"), sem("wB_ready")
    t_mm, t_ready = sem("t_mm"), sem("t_ready")
    c_mm, c_hi, c_ready = sem("c_mm"), sem("c_hi"), sem("c_ready")
    q_mm, q_hi, q_ready = sem("q_mm"), sem("q_hi"), sem("q_ready")
    e_mm, e_hi, e_free = sem("e_mm"), sem("e_hi"), sem("e_free")
    f_mm, f_hi, f_free = sem("f_mm"), sem("f_hi"), sem("f_free")
    stage_out = sem("stage_out")

    def kq(w, j, qt):
        return w[:, (j * QT + qt) * P:(j * QT + qt + 1) * P]

    def qrw(w, j, qt):
        return w[:, W_KQ + (j * QT + qt) * R:W_KQ + (j * QT + qt + 1) * R]

    def wq(w, j, c):
        at = W_KQ + W_QR + j * D + c * P
        return w[:, at:at + P]

    block = ctx.enter_context(nc.Block())

    @block.sync
    def _(sp):
        for a in range(XP):
            part = slice(a * NT // XP, (a + 1) * NT // XP)
            sp.dma_start(x_all[:, part, :], x_d[part].rearrange("t p c -> p t c")).then_inc(x_in[a], 16)
        for j in range(2):
            sp.dma_start(raw[j][:], w_pairs[j]).then_inc(w_in[j], 16)
        sp.sem_inc(stage_out, 32)

        def step(p, j, more):
            if more:
                sp.wait_ge(c_mm, p + 1)
                sp.wait_ge(wB_ready, p + 1)
                sp.dma_start(raw[j][:], w_pairs[p + 2]).then_inc(w_in[j], 16)
            sp.wait_ge(e_free, 4 * p + 4 + 2)
            for a in range(2):
                sp.dma_start(qe_d[a, :, :, p, :].rearrange("b d x -> d b x"),
                             stage_o[:, a]).then_inc(stage_out, 16)

        with sp.Fori(0, NP // 2 - 1) as i:
            for j in range(2):
                step(2 * i + j, j, True)
        for j in range(2):
            step(NP - 2 + j, j, False)
        sp.wait_ge(stage_out, 32 * (NP + 1))

    @block.gpsimd
    def _(pool):
        pool.memset(ident[:], 0.0).then_inc(const_set, 1)
        pool.memset(eps_pow[:], -0.5).then_inc(const_set, 1)
        pool.wait_ge(const_set, 2)
        pool.affine_select(out=ident[:], in_=ident[:], compare_op=ALU.not_equal, fill=1.0, base=0,
                           pattern=[[-1, P]], channel_multiplier=1).then_inc(const_set, 1)
        pool.wait_ge(ln1, NT + NT + 1)
        pool.tensor_tensor(rstd[:], var[:], eps_pow[:, 0:1].to_broadcast([P, NT]),
                           ALU.pow).then_inc(rstd1, 1)

        def split_low(j, q):
            pool.wait_ge(wB_hi, q + 1)
            pool.tensor_tensor(WB[j].lo[:], raw[j][:, W_A:], f32(WB[j].hi[:]), ALU.subtract).then_inc(wB_ready, 1)

        with pool.Fori(0, NP // 2) as i:
            for j in range(2):
                split_low(j, 2 * i + j)

    @block.scalar
    def _(act):
        def split_high(j, n):
            act.wait_ge(w_in[j], 16 * n)
            act.copy(WB[j].hi[:], raw[j][:, W_A:]).then_inc(wB_hi, 1)

        def fold_t(q):
            act.wait_ge(t_mm, q + 1)
            act.copy(TW[:].rearrange("p j r -> p (j r)"), psT[:, 0:2 * R]).then_inc(t_ready, 1)

        def fold_c(q):
            act.wait_ge(c_mm, q + 1)
            act.copy(C.hi[:].rearrange("p k m -> p (k m)"), psC[:]).then_inc(c_hi, 1)

        for tt in range(NT):
            act.wait_ge(h1_turned, tt + 1)
            act.copy(h1T.hi[:, :, tt * P:(tt + 1) * P],
                     (psE if tt % 2 else psQ)[:, 0, :].rearrange("p (k t) -> p k t", k=KC)).then_inc(h1_hi, 1)
            if tt == T_AT:
                fold_t(0)
            if tt == C_AT:
                fold_c(0)
        split_high(0, 1)
        split_high(1, 1)

        def step(p, j, ahead, ahead2, n):
            for half in range(2):
                act.wait_ge(q_mm, 2 * p + half + 1)
                act.copy(Q.hi[:, half * BANK:(half + 1) * BANK], psQ[:, half]).then_inc(q_hi, 1)
            if ahead:
                fold_t(p + 1)
            act.wait_ge(stage_out, 32 * p + 32)
            for jj in range(2):
                for half in range(2):
                    act.wait_ge(e_mm, 4 * p + 2 * jj + half + 1)
                    act.copy(stage_w[:, 0, half * B // 2:(half + 1) * B // 2, jj, :],
                             psE[:, half].rearrange("p (b s) -> p b s", s=S)).then_inc(e_hi, 1)
                if ahead and jj == 0:
                    fold_c(p + 1)
            for jj in range(2):
                act.wait_ge(f_mm, 2 * p + jj + 1)
                act.copy(F.hi[:, bass.ds(2 * p + jj, 1), :], psF[:, jj:jj + 1]).then_inc(f_hi, 1)
            if ahead2:
                split_high(j, n)

        with act.Fori(0, NP // 2 - 1) as i:
            for j in range(2):
                step(2 * i + j, j, True, True, i + 2)
        step(NP - 2, 0, True, False, 0)
        step(NP - 1, 1, False, False, 0)

    @block.vector
    def _(dve):
        dve.sem_inc(e_free, 2)
        dve.sem_inc(f_free, 2)
        for tt in range(NT):
            dve.wait_ge(x_in[tt * XP // NT], 16)
            dve.bn_stats(st[:, tt, :], x_all[:, tt, :]).then_inc(ln1, 1)
            dve.wait_ge(ln1, 2 * tt + 1)
            dve.bn_aggr(mv[:, tt, :], st[:, tt, :]).then_inc(ln1, 1)
        dve.wait_ge(ln1, 2 * NT)
        dve.tensor_scalar(var[:], mv[:, :, 1], EPS, None, ALU.add).then_inc(ln1, 1)

        def norm(tt):
            if tt >= 2:
                dve.wait_ge(h1_turned, tt - 1)
            dve.tensor_scalar(h[tt % 2][:], x_all[:, tt, :], mv[:, tt, 0:1], rstd[:, tt:tt + 1],
                              ALU.subtract, ALU.mult).then_inc(h1_made, 1)

        def fold_c(q):
            dve.wait_ge(c_hi, q + 1)
            dve.tensor_tensor(C.lo[:].rearrange("p k m -> p (k m)"), psC[:],
                              f32(C.hi[:].rearrange("p k m -> p (k m)")), ALU.subtract).then_inc(c_ready, 1)

        dve.wait_ge(rstd1, 1)
        for tt in range(2):
            norm(tt)
        for tt in range(NT):
            dve.wait_ge(h1_hi, tt + 1)
            dst = slice(tt * P, (tt + 1) * P)
            dve.tensor_tensor(h1T.lo[:, :, dst], (psE if tt % 2 else psQ)[:, 0, :].rearrange("p (k t) -> p k t", k=KC),
                              f32(h1T.hi[:, :, dst]), ALU.subtract).then_inc(h1_lo, 1)
            if tt + 2 < NT:
                norm(tt + 2)
            if tt == C_AT:
                fold_c(0)

        def step(p, ahead):
            for half in range(2):
                cols = slice(half * BANK, (half + 1) * BANK)
                dve.wait_ge(q_hi, 2 * p + half + 1)
                dve.tensor_tensor(Q.lo[:, cols], psQ[:, half], f32(Q.hi[:, cols]),
                                  ALU.subtract).then_inc(q_ready, 1)
            for jj in range(2):
                for half in range(2):
                    bs = slice(half * B // 2, (half + 1) * B // 2)
                    dve.wait_ge(e_hi, 4 * p + 2 * jj + half + 1)
                    dve.tensor_tensor(stage_w[:, 1, bs, jj, :], psE[:, half].rearrange("p (b s) -> p b s", s=S),
                                      f32(stage_w[:, 0, bs, jj, :]), ALU.subtract).then_inc(e_free, 1)
                if ahead and jj == 0:
                    fold_c(p + 1)
            for jj in range(2):
                dve.wait_ge(f_hi, 2 * p + jj + 1)
                dst = bass.ds(2 * p + jj, 1)
                dve.tensor_tensor(F.lo[:, dst, :], psF[:, jj:jj + 1], f32(F.hi[:, dst, :]),
                                  ALU.subtract).then_inc(f_free, 1)

        with dve.Fori(0, NP // 2 - 1) as i:
            for j in range(2):
                step(2 * i + j, True)
        step(NP - 2, True)
        step(NP - 1, False)

    @block.tensor
    def _(pe):
        pe.wait_ge(const_set, 3)
        def fold_t(j, n):
            pe.wait_ge(w_in[j], 16 * n)
            for jj in range(2):
                for qt in range(QT):
                    last = pe.matmul(psT[:, jj * R:(jj + 1) * R], kq(raw[j], jj, qt), qrw(raw[j], jj, qt),
                                     start=qt == 0, stop=qt == QT - 1, skip_group_check=True)
            last.then_inc(t_mm, 1)

        def fold_c(q, j):
            pe.wait_ge(t_ready, q + 1)
            for c in range(KC):
                for jj in range(2):
                    at = c * P + jj * R
                    last = pe.matmul(psC[:, at:at + R], wq(raw[j], jj, c), TW[:, jj, :], start=True, stop=True,
                                     skip_group_check=True)
            last.then_inc(c_mm, 1)

        for tt in range(NT):
            pe.wait_ge(h1_made, tt + 1)
            if tt >= 2:
                pe.wait_ge(h1_lo, tt - 1)
            for k in range(KC):
                last = pe.transpose((psE if tt % 2 else psQ)[:, 0, k * P:(k + 1) * P],
                                    h[tt % 2][:, k * P:(k + 1) * P], ident[:])
            last.then_inc(h1_turned, 1)
            if tt == T_AT:
                fold_t(0, 1)
            if tt == C_AT:
                fold_c(0, 0)
        pe.wait_ge(h1_lo, NT)

        def step(p, j, ahead, n):
            pe.wait_ge(c_ready, p + 1)
            for half in range(2):
                for k in range(KC):
                    last = mm3(pe, psQ[:, half], C.at(ALL, k, ALL),
                               h1T.at(ALL, k, slice(half * BANK, (half + 1) * BANK)), k == 0, k == KC - 1)
                last.then_inc(q_mm, 1)
            if ahead:
                fold_t(1 - j, n)
            pe.wait_ge(wB_ready, p + 1)
            for jj in range(2):
                rows = slice(jj * R, (jj + 1) * R)
                for half in range(2):
                    pe.wait_ge(q_ready, 2 * p + half + 1)
                    pe.wait_ge(e_free, 4 * p + 2 * jj + half + 1)
                    mm3(pe, psE[:, half], WB[j].at(rows, slice(0, W_KR)),
                        Q.at(rows, slice(half * BANK, (half + 1) * BANK)), True, True).then_inc(e_mm, 1)
                if ahead and jj == 0:
                    fold_c(p + 1, 1 - j)
            for jj in range(2):
                pe.wait_ge(f_free, 2 * p + jj + 1)
                kv, wo = W_KR + jj * DC, W_KR + W_KV + jj * D
                mm3(pe, psF[:, jj], WB[j].at(ALL, slice(kv, kv + DC)), WB[j].at(ALL, slice(wo, wo + D)),
                    True, True).then_inc(f_mm, 1)

        with pe.Fori(0, NP // 2 - 1) as i:
            for j in range(2):
                step(2 * i + j, j, True, i + 1 + j)
        step(NP - 2, 0, True, NP // 2)
        step(NP - 1, 1, False, 0)


HALVES = 2
RT = H * S // HALVES // P
HB = 2 * HALVES
PTN = 4
K_STEPS, R_STEP = (2, 6), 4


def turn_order(hf, has_k):
    out = []
    for k in range(LT):
        out.append(("P", k))
        if hf == 0 and has_k and k in K_STEPS:
            out.append(("K", K_STEPS.index(k)))
        if k == R_STEP:
            out.append(("R", 0))
    return out


def turn_counts(has_k):
    at, split = {}, 0
    for hf in range(HALVES):
        for what in turn_order(hf, has_k):
            at[(hf, *what)] = (len(at), split)
            split += what[0] != "R"
    return at


TURNS, SPLITS = len(turn_counts(True)), sum(w[1] != "R" for w in turn_counts(True))


def build_cross(nc, ctx, sem, t, keep):
    ident, F, eps_pow = keep["ident"], keep["F"], keep["eps_pow"]
    kv_d, x_d, x1_d, h2_d = t["ctx"], t["x"], t["x1"], t["h2T"]
    qe_d = t["qe"].rearrange("a b d p x -> b d a (p x)")

    def sb(name, shape, dt=F32):
        return ctx.enter_context(nc.sbuf_tensor(name, shape, dt))

    tab = sb("rope_tab", [P, 2, LT * DC // 2])
    kv = sb("kv_raw", [P, LT * DC])
    kr = sb("kv_rope", [P, LT * DC])
    kt = sb("kv_turned_term", [P, LT * DC])
    KV = [Pair(ctx, nc, f"kv{j}", [P, LT, DC]) for j in range(2)]
    KT = [Pair(ctx, nc, f"kT{j}", [P, L]) for j in range(2)]
    QE = [ctx.enter_context(nc.sbuf_tensor(f"qe{j}", [P, 2, H * S], F32R)) for j in range(2)]
    PR = [sb(f"probs{j}", [P, RT, L]) for j in range(2)]
    PT = [Pair(ctx, nc, f"probsT{j}", [P, BANK]) for j in range(PTN)]
    CT = Pair(ctx, nc, "ctxT", [P, H, P])
    CX = sb("ctx_f32", [P, BANK])
    RB = sb("recip_rows", [P, BANK])
    XT, X1, HN = sb("x_tile", [P, D]), sb("x1_tile", [P, D]), sb("h2_tile", [P, D])
    H2 = sb("h2T_tile", [P, 2, D])
    nmax = [sb(f"nmax{j}", [P, RT]) for j in range(2)]
    rsum = [sb(f"rsum{j}", [P, RT]) for j in range(2)]
    rinv = sb("rinv", [P, RT])
    st, mv, var, rstd = sb("st2", [P, 6]), sb("mv2", [P, 2]), sb("var2", [P, 1]), sb("rstd2", [P, 1])

    psS = [ctx.enter_context(nc.psum_tensor(f"psS{j}", [P, L], F32)) for j in range(2)]
    psT = [ctx.enter_context(nc.psum_tensor(f"psTr{j}", [P, BANK], F32)) for j in range(2)]
    psV = ctx.enter_context(nc.psum_tensor("psV", [P, BANK], F32))
    psX = ctx.enter_context(nc.psum_tensor("psX", [P, BANK], F32))

    tab_in, kv_in, xt_in = sem("tab_in"), sem("kv_in"), sem("xt_in")
    qe_in = [sem(f"qe_in{j}") for j in range(2)]
    rope_part, rope_done = sem("rope_part"), sem("rope_done")
    kv_hi, kv_lo = sem("kv_hi"), sem("kv_lo")
    turned, turned_hi, turned_free = sem("turned"), sem("turned_hi"), sem("turned_free")
    recip_made, rows_made = sem("recip_made"), sem("rows_made")
    s_mm, max_made, exp_done = sem("s_mm"), sem("max_made"), sem("exp_done")
    pv_done = sem("pv_done")
    cx_done, ct_hi, ct_lo = sem("cx_done"), sem("ct_hi"), sem("ct_lo")
    proj_done, x1_made = sem("proj_done"), sem("x1_made")
    ln2, ln2_seen, rstd2, h2_made = sem("ln2"), sem("ln2_seen"), sem("rstd2"), sem("h2_made")
    h2_turned, h2_hi, h2_lo = sem("h2_turned"), sem("h2_hi"), sem("h2_lo")
    x1_out, h2_out = sem("x1_out"), sem("h2_out")

    AT = {True: turn_counts(True), False: turn_counts(False)}

    def place(b, hf, what, k, has_k):
        g, m = AT[has_k][(hf, what, k)]
        return 2 + TURNS * b + g + 1, 2 + SPLITS * b + m + 1, 2 + SPLITS * b + m + 1 + 2

    def half_steps(i, c, first, last):
        n, b = HB * i + c, 2 * i + c // 2
        has_k = not (last and c >= 2)
        more = not (last and c == 3)
        return n, b, c // 2, c % 2, has_k, more

    block = ctx.enter_context(nc.Block())

    @block.sync
    def _(sp):
        sp.dma_start(tab[:], t["rope_x"]).then_inc(tab_in, 16)

        def load(b, j, i, first):
            sp.wait_ge(rope_done, b + 1)
            sp.dma_start(kv[:], kv_d[b]).then_inc(kv_in, 16)
            if not first:
                sp.wait_ge(s_mm, 8 * b - 8)
            sp.dma_start(QE[j][:].bitcast(F32), qe_d[b]).then_inc(qe_in[j], 16)
            if j == 1:
                sp.wait_ge(x1_made, i + 1)
                sp.dma_start(XT[:], x_d[i]).then_inc(xt_in, 16)

        for j in range(2):
            load(j, j, 0, True)
        with sp.Fori(1, B // 2) as i:
            for j in range(2):
                load(2 * i + j, j, i, False)

    @block.gpsimd
    def _(pool):
        pool.sem_inc(rope_done, 1)
        pool.sem_inc(ct_lo, 1)

        def rope(b):
            pool.wait_ge(kv_in, 16 * b + 16)
            pool.wait_ge(rope_done, b + 1)
            pair = lambda ap, n: ap.rearrange("p (a two) -> p a two", two=2)
            cos = tab[:, 0, :].unsqueeze(2).to_broadcast([P, LT * DC // 2, 2])
            pool.tensor_tensor(pair(kr[:], 2), pair(kv[:], 2), cos, ALU.mult).then_inc(rope_part, 1)
            quarter = DC // 4
            for half in range(2):
                dst = kt[:].rearrange("p (l h a two) -> p l h a two", h=2, a=quarter, two=2)[:, :, half]
                src = kv[:].rearrange("p (l h a two) -> p l h a two", h=2, a=quarter, two=2)[:, :, 1 - half]
                sin = tab[:, 1, :].rearrange("p (l h a) -> p l h a", h=2, a=quarter)[:, :, half, :]
                pool.tensor_tensor(dst, src, sin.unsqueeze(3).to_broadcast([P, LT, quarter, 2]),
                                   ALU.mult).then_inc(rope_part, 1)
            pool.wait_ge(rope_part, 3 * b + 3)
            pool.tensor_tensor(kr[:], kr[:], kt[:], ALU.add).then_inc(rope_done, 1)

        def kv_low(b, j):
            pool.wait_ge(kv_hi, b + 1)
            pool.tensor_tensor(KV[j].lo[:].rearrange("p l d -> p (l d)"), kr[:],
                               f32(KV[j].hi[:].rearrange("p l d -> p (l d)")), ALU.subtract).then_inc(kv_lo, 1)

        def ctx_low(n, c):
            cols = (slice((c % 2) * H // 2, (c % 2 + 1) * H // 2), slice((c // 2) * S, (c // 2 + 1) * S))
            pool.wait_ge(ct_hi, n + 1)
            pool.tensor_tensor(CT.lo[:, cols[0], cols[1]], CX[:].rearrange("p (h s) -> p h s", s=S),
                               f32(CT.hi[:, cols[0], cols[1]]), ALU.subtract).then_inc(ct_lo, 1)

        def root(tt):
            pool.wait_ge(ln2, 3 * tt + 3)
            pool.tensor_tensor(rstd[:], var[:], eps_pow[:], ALU.pow).then_inc(rstd2, 1)

        pool.wait_ge(tab_in, 16)
        rope(0)
        kv_low(0, 0)
        pool.wait_ge(turned, 2)
        pool.wait_ge(kv_lo, 1)
        rope(1)

        def iteration(i, first, last):
            for c in range(HB):
                n, b, j, hf, has_k, more = half_steps(i, c, first, last)
                if not (first and c == 0):
                    ctx_low(n - 1, (c - 1) % HB)
                if c == 1 and not first:
                    root(i - 1)
                if hf == 0 and has_k:
                    kv_low(b + 1, 1 - j)
                if hf == 1 and not last:
                    pool.wait_ge(turned, place(b, 0, "K", 1, True)[0])
                    pool.wait_ge(kv_lo, b + 2)
                    rope(b + 2)

        iteration(0, True, False)
        with pool.Fori(1, NT - 1) as i:
            iteration(i, False, False)
        iteration(NT - 1, False, True)
        ctx_low(HB * NT - 1, HB - 1)
        root(NT - 1)

    @block.scalar
    def _(act):
        act.sem_inc(exp_done, 2)
        act.sem_inc(x1_out, 16)
        act.sem_inc(h2_out, 16)

        def kv_high(b, j):
            act.wait_ge(rope_done, b + 2)
            act.copy(KV[j].hi[:].rearrange("p l d -> p (l d)"), kr[:]).then_inc(kv_hi, 1)

        def exps(n, np_, rt):
            act.wait_ge(max_made, RT * n + rt + 1)
            act.activation(PR[np_][:, rt, :], psS[rt % 2][:], ACT.Exp, bias=nmax[np_][:, rt:rt + 1],
                           accum_out=rsum[np_][:, rt:rt + 1]).then_inc(exp_done, 1)

        def ctx_high(n, c, i):
            act.wait_ge(cx_done, n + 2)
            if c == 0:
                act.wait_ge(proj_done, i + 1)
            act.copy(CT.hi[:, (c % 2) * H // 2:(c % 2 + 1) * H // 2, (c // 2) * S:(c // 2 + 1) * S],
                     CX[:].rearrange("p (h s) -> p h s", s=S)).then_inc(ct_hi, 1)

        def store_x1(tt):
            act.wait_ge(x1_made, tt + 2)
            act.dma_start(x1_d[tt], X1[:]).then_inc(x1_out, 16)

        def h2_high(tt):
            act.wait_ge(h2_turned, tt + 1)
            act.wait_ge(h2_out, 16 * tt + 16)
            act.copy(H2[:, 0, :].bitcast(F32R), psX[:]).then_inc(h2_hi, 1)

        def store_h2(tt):
            act.wait_ge(h2_lo, tt + 2)
            act.dma_start(h2_d[tt], H2[:]).then_inc(h2_out, 16)

        for k in range(2):
            act.wait_ge(turned, k + 1)
            act.copy(KT[0].hi[:, k * BANK:(k + 1) * BANK], psT[k][:]).then_inc(turned_hi, 1)
        kv_high(0, 0)
        for rt in range(RT):
            exps(0, 0, rt)

        def iteration(i, first, last):
            for c in range(HB):
                n, b, j, hf, has_k, more = half_steps(i, c, first, last)
                for k in range(LT):
                    g = place(b, hf, "P", k, has_k)
                    slot = AT[has_k][(hf, "P", k)][0] % 2
                    act.wait_ge(turned, g[0])
                    act.wait_ge(pv_done, LT * n + k + 1)
                    act.copy(PT[k % PTN].hi[:], psT[slot][:]).then_inc(turned_hi, 1)
                    if hf == 0 and has_k and k in K_STEPS:
                        q = K_STEPS.index(k)
                        slot = AT[True][(0, "K", q)][0] % 2
                        act.wait_ge(turned, place(b, 0, "K", q, True)[0])
                        act.copy(KT[1 - j].hi[:, q * BANK:(q + 1) * BANK], psT[slot][:]).then_inc(turned_hi, 1)
                    if k == 1 and not (first and c == 0):
                        ctx_high(n - 1, (c - 1) % HB, i)
                    if k == 3 and hf == 0 and has_k:
                        kv_high(b + 1, 1 - j)
                    if k == R_STEP:
                        g = place(b, hf, "R", 0, has_k)
                        slot = AT[has_k][(hf, "R", 0)][0] % 2
                        act.wait_ge(turned, g[0])
                        act.copy(RB[:], psT[slot][:]).then_inc(rows_made, 1)
                    if k % 2 == 1 and more:
                        exps(n + 1, (c + 1) % 2, k // 2)
                    if not first:
                        if (c, k) == (1, 5):
                            store_x1(i - 1)
                        if (c, k) == (2, 6):
                            h2_high(i - 1)
                        if (c, k) == (3, 1):
                            store_h2(i - 1)

        iteration(0, True, False)
        with act.Fori(1, NT - 1) as i:
            iteration(i, False, False)
        iteration(NT - 1, False, True)
        ctx_high(HB * NT - 1, HB - 1, NT - 1)
        store_x1(NT - 1)
        h2_high(NT - 1)
        store_h2(NT - 1)
        act.wait_ge(x1_out, 16 * NT + 16)
        act.wait_ge(h2_out, 16 * NT + 16)

    @block.vector
    def _(dve):
        dve.sem_inc(turned_free, 2)
        dve.sem_inc(cx_done, 1)
        dve.sem_inc(x1_made, 1)
        dve.sem_inc(h2_lo, 1)

        def maxes(n, np_, rt):
            dve.wait_ge(s_mm, RT * n + rt + 1)
            dve.tensor_reduce(nmax[np_][:, rt:rt + 1], psS[rt % 2][:], AX.X, ALU.max,
                              negate=True).then_inc(max_made, 1)

        def lo_part(hi_count, out, slot, hi):
            dve.wait_ge(turned_hi, hi_count)
            dve.tensor_tensor(out, psT[slot][:], f32(hi), ALU.subtract).then_inc(turned_free, 1)

        def residual(tt):
            dve.wait_ge(proj_done, tt + 2)
            dve.wait_ge(xt_in, 16 * tt + 16)
            dve.wait_ge(x1_out, 16 * tt + 16)
            dve.tensor_tensor(X1[:], psX[:], XT[:], ALU.add).then_inc(x1_made, 1)

        def stats(tt):
            dve.wait_ge(x1_made, tt + 2)
            dve.bn_stats(st[:], X1[:]).then_inc(ln2, 1)

        def aggregate(tt):
            dve.wait_ge(ln2, 3 * tt + 1)
            dve.sem_inc(ln2_seen, 1)
            dve.bn_aggr(mv[:], st[:]).then_inc(ln2, 1)

        def variance(tt):
            dve.wait_ge(ln2, 3 * tt + 2)
            dve.tensor_scalar(var[:], mv[:, 1:2], EPS, None, ALU.add).then_inc(ln2, 1)

        def norm(tt):
            dve.wait_ge(rstd2, tt + 1)
            dve.tensor_scalar(HN[:], X1[:], mv[:, 0:1], rstd[:], ALU.subtract, ALU.mult).then_inc(h2_made, 1)

        def h2_low(tt):
            dve.wait_ge(h2_hi, tt + 1)
            dve.tensor_tensor(H2[:, 1, :].bitcast(F32R), psX[:], H2[:, 0, :], ALU.subtract).then_inc(h2_lo, 1)

        LN_STEPS = {1: residual, 3: stats, 4: aggregate, 5: variance}

        for k in range(2):
            cols = slice(k * BANK, (k + 1) * BANK)
            lo_part(k + 1, KT[0].lo[:, cols], k, KT[0].hi[:, cols])
        for rt in range(RT):
            maxes(0, 0, rt)

        def iteration(i, first, last):
            for c in range(HB):
                n, b, j, hf, has_k, more = half_steps(i, c, first, last)
                for k in range(LT):
                    g = place(b, hf, "P", k, has_k)
                    lo_part(g[1], PT[k % PTN].lo[:], AT[has_k][(hf, "P", k)][0] % 2, PT[k % PTN].hi[:])
                    if k == 2:
                        dve.wait_ge(exp_done, RT * n + RT + 2)
                        dve.reciprocal(rinv[:], rsum[c % 2][:]).then_inc(recip_made, 1)
                    if k % 2 == 0 and more:
                        maxes(n + 1, (c + 1) % 2, k // 2)
                    if hf == 0 and has_k and k in K_STEPS:
                        q = K_STEPS.index(k)
                        cols = slice(q * BANK, (q + 1) * BANK)
                        lo_part(place(b, 0, "K", q, True)[1], KT[1 - j].lo[:, cols],
                                AT[True][(0, "K", q)][0] % 2, KT[1 - j].hi[:, cols])
                    if not first:
                        if c == 1 and k in LN_STEPS:
                            LN_STEPS[k](i - 1)
                        if (c, k) == (2, 1):
                            norm(i - 1)
                        if (c, k) == (2, 7):
                            h2_low(i - 1)
                dve.wait_ge(rows_made, n + 1)
                dve.wait_ge(pv_done, LT * n + LT + PTN)
                dve.wait_ge(ct_lo, n + 1)
                dve.tensor_tensor(CX[:], psV[:], RB[:], ALU.mult).then_inc(cx_done, 1)

        iteration(0, True, False)
        with dve.Fori(1, NT - 1) as i:
            iteration(i, False, False)
        iteration(NT - 1, False, True)
        for part in LN_STEPS.values():
            part(NT - 1)
        norm(NT - 1)
        h2_low(NT - 1)

    @block.tensor
    def _(pe):
        pe.sem_inc(pv_done, PTN)
        pe.sem_inc(proj_done, 1)

        def scores(n, j, hf, rt):
            pe.wait_ge(exp_done, RT * n + rt + 1)
            rows = slice(hf * BANK + rt * P, hf * BANK + (rt + 1) * P)
            for half in range(2):
                cols = slice(half * BANK, (half + 1) * BANK)
                last = mm3(pe, psS[rt % 2][:, cols], (QE[j][:, 0, rows], QE[j][:, 1, rows]),
                           KT[j].at(ALL, cols), True, True)
            last.then_inc(s_mm, 1)

        def turn(slot, src):
            for q in range(BANK // P):
                last = pe.transpose(psT[slot][:, q * P:(q + 1) * P], src(q), ident[:])
            last.then_inc(turned, 1)

        def slot_free(b, hf, what, k, has_k):
            at = AT[has_k]
            g = at[(hf, what, k)][0]
            if g < 2:
                pe.wait_ge(turned_free, 2 + SPLITS * b + g - 2 + 1 + 2)
            else:
                before = next(w for w in at if at[w][0] == g - 2)
                if before[1] == "R":
                    pe.wait_ge(rows_made, HALVES * b + before[0] + 1)
                else:
                    pe.wait_ge(turned_free, place(b, *before, has_k)[2])
            return g % 2

        def project(tt, heads):
            for h in heads:
                if h == 0:
                    pe.wait_ge(h2_lo, tt + 1)
                    pe.wait_ge(ct_lo, HB * tt + HB)
                if h == H // 2:
                    pe.wait_ge(ct_lo, HB * tt + HB + 1)
                last = mm3(pe, psX[:], CT.at(ALL, h, ALL), F.at(ALL, h, ALL), h == 0, h == H - 1)
            if h == H - 1:
                last.then_inc(proj_done, 1)

        def turn_h2(tt):
            pe.wait_ge(h2_made, tt + 1)
            for k in range(KC):
                last = pe.transpose(psX[:, k * P:(k + 1) * P], HN[:, k * P:(k + 1) * P], ident[:])
            last.then_inc(h2_turned, 1)

        pe.wait_ge(rope_done, 2)
        for k in range(2):
            turn(k, lambda q: kr[:, (4 * k + q) * P:(4 * k + q + 1) * P])
        pe.wait_ge(turned_free, 4)
        pe.wait_ge(qe_in[0], 16)
        for rt in range(RT):
            scores(0, 0, 0, rt)

        def iteration(i, first, last):
            for c in range(HB):
                n, b, j, hf, has_k, more = half_steps(i, c, first, last)
                for k in range(LT):
                    if k == 0:
                        pe.wait_ge(exp_done, RT * n + RT + 2)
                    turn(slot_free(b, hf, "P", k, has_k), lambda q: PR[c % 2][:, q, k * P:(k + 1) * P])
                    if k % 2 == 0 and more:
                        if hf == 1 and k == 0:
                            pe.wait_ge(turned_free, place(b, 0, "K", 1, True)[2])
                            pe.wait_ge(qe_in[1 - j], 16 * (i + 1 + j))
                        scores(n + 1, j if hf == 0 else 1 - j, 1 - hf, k // 2)
                    if hf == 0 and has_k and k in K_STEPS:
                        at = 4 * K_STEPS.index(k)
                        if at == 0:
                            pe.wait_ge(rope_done, b + 3)
                        turn(slot_free(b, 0, "K", at // 4, True), lambda q: kr[:, (at + q) * P:(at + q + 1) * P])
                    if k == R_STEP:
                        pe.wait_ge(recip_made, n + 1)
                        turn(slot_free(b, hf, "R", 0, has_k), lambda q: rinv[:, q:q + 1].to_broadcast([P, P]))
                    for kk in ([k - 2] if k in range(2, LT - 1) else [LT - 3, LT - 2, LT - 1] if k == LT - 1 else []):
                        pe.wait_ge(turned_free, place(b, hf, "P", kk, has_k)[2])
                        if kk == 0:
                            pe.wait_ge(cx_done, n + 1)
                            pe.wait_ge(kv_lo, b + 1)
                        mm3(pe, psV[:], KV[j].at(ALL, kk, ALL), PT[kk % PTN].at(ALL, ALL),
                            kk == 0, kk == LT - 1).then_inc(pv_done, 1)
                    if not first:
                        if c == 0:
                            project(i - 1, range(2 * k, 2 * k + 2))
                        if (c, k) == (2, 5):
                            turn_h2(i - 1)

        iteration(0, True, False)
        with pe.Fori(1, NT - 1) as i:
            iteration(i, False, False)
        iteration(NT - 1, False, True)
        project(NT - 1, range(H))
        turn_h2(NT - 1)


NGRP = NT * HKV
WCH = 5
GI = 2 * HKV


def wait(eng, sem, value):
    if not isinstance(value, int) or value > 0:
        eng.wait_ge(sem, value)


def build_self(nc, ctx, sem, t, keep):
    ident = keep["ident"]

    def sb(name, shape, dt=F32):
        return ctx.enter_context(nc.sbuf_tensor(name, shape, dt))

    W = Pair(ctx, nc, "wqkv", [P, WCH, KC, BANK])
    raw = [sb(f"wqkv_raw{c}", [P, KC, BANK]) for c in range(WCH)]
    tab = sb("rope_s_tab", [P, 2, 3, DH // 2])
    mask_f, mask = sb("mask_f", [P, BANK]), sb("mask_r", [P, BANK], F32R)
    ident_r = sb("ident_r", [P, P], F32R)
    HT = [sb(f"h2T{j}", [P, 2, KC, P], F32R) for j in range(2)]
    QR = sb("q_terms", [P, 2, BANK])
    KR = sb("k_terms", [P, 2, HKV * DH])
    QN, KN = sb("q_rope", [P, BANK]), sb("k_rope", [P, HKV, 2, DH])
    QT2 = [sb(f"qT{j}", [P, KC, P]) for j in range(2)]
    KT = sb("kTs", [P, HKV, P])
    VZ = Pair(ctx, nc, "v_padded", [P, HKV, 3 * DH])
    PR = [sb(f"sprobs{j}", [P, REP, P]) for j in range(2)]
    PT = [Pair(ctx, nc, f"sprobsT{j}", [P, REP, P]) for j in range(2)]
    AO = [sb(f"attn_out{j}", [P, BANK]) for j in range(2)]
    nmax = [sb(f"snmax{j}", [P, REP]) for j in range(2)]
    rsum = [sb(f"srsum{j}", [P, REP]) for j in range(2)]
    rinv = [sb(f"srinv{j}", [P, REP]) for j in range(2)]

    psS = ctx.enter_context(nc.psum_tensor("psSs", [P, REP, P], F32))
    psP = ctx.enter_context(nc.psum_tensor("psP", [P, REP, P], F32))
    psQ = ctx.enter_context(nc.psum_tensor("psQs", [P, BANK], F32))
    psK = ctx.enter_context(nc.psum_tensor("psK", [P, BANK], F32))
    psT = ctx.enter_context(nc.psum_tensor("psTq", [P, BANK], F32))
    psO = ctx.enter_context(nc.psum_tensor("psO", [P, BANK], F32))

    w_in = [sem(f"wqkv_in{c}") for c in range(WCH)]
    tab_in = sem("tabs_in")
    ht_in = [sem(f"ht_in{j}") for j in range(2)]
    w_hi, w_ready = sem("wqkv_hi"), sem("wqkv_ready")
    zeroed, consts = sem("zeroed"), sem("consts")
    kv_mm, q_mm = sem("skv_mm"), sem("sq_mm")
    k_terms, q_terms, k_roped, q_roped = sem("k_terms"), sem("q_terms"), sem("k_roped"), sem("q_roped")
    t_mm, t_out = sem("st_mm"), sem("st_out")
    v_hi, v_lo = sem("sv_hi"), sem("sv_lo")
    s_mm, max_made, exp_done = sem("ss_mm"), sem("smax_made"), sem("sexp_done")
    recip_made, normed = sem("srecip_made"), sem("normed")
    p_mm, p_hi, p_lo = sem("sp_mm"), sem("sp_hi"), sem("sp_lo")
    pv_mm, ao_made = sem("spv_mm"), sem("ao_made")
    ao_out = [sem(f"ao_out{j}") for j in range(2)]

    def order_k(tt):
        return (HKV + 1) * tt

    def order_q(tt, g):
        return (HKV + 1) * tt + g + 1

    def halves(ap):
        return ap.rearrange("p (h two x) -> p h two x", two=2, x=DH // 2)

    def plan(i, v, last):
        def ahead(k):
            return not last or v + k < GI
        return GI * i + v, 2 * i + v // HKV, v % HKV, ahead

    def turns(eng, step):
        for v in range(GI):
            step(0, v, False)
        with eng.Fori(1, NT // 2 - 1) as i:
            for v in range(GI):
                step(i, v, False)
        for v in range(GI):
            step(NT // 2 - 1, v, True)

    block = ctx.enter_context(nc.Block())

    @block.sync
    def _(sp):
        sp.dma_start(raw[0][:], t["w_qkv"][0]).then_inc(w_in[0], 16)
        sp.dma_start(HT[0][:].bitcast(F32).rearrange("p a k x -> p a (k x)"), t["h2T"][0]).then_inc(ht_in[0], 16)
        sp.dma_start(tab[:], t["rope_s"]).then_inc(tab_in, 16)
        sp.dma_start(mask_f[:], t["mask"]).then_inc(tab_in, 16)
        for c in range(1, WCH):
            sp.dma_start(raw[c][:], t["w_qkv"][c]).then_inc(w_in[c], 16)
        sp.dma_start(HT[1][:].bitcast(F32).rearrange("p a k x -> p a (k x)"), t["h2T"][1]).then_inc(ht_in[1], 16)

        def step(i, v, last):
            u, tt, g, ahead = plan(i, v, last)
            if g == 2 and ahead(GI):
                sp.wait_ge(q_mm, u + 2)
                sp.dma_start(HT[v // HKV][:].bitcast(F32).rearrange("p a k x -> p a (k x)"),
                             t["h2T"][tt + 2]).then_inc(ht_in[v // HKV], 16)
            if not (isinstance(u, int) and u == 0):
                store(u - 1, tt if g else tt - 1, (g - 1) % HKV, (v - 1) % 2)

        def store(u, tt, g, j):
            sp.wait_ge(ao_made, u + 1)
            sp.dma_start(t["ao"][tt, :, g * KC:(g + 1) * KC, :],
                         AO[j][:].rearrange("p (a x) -> p a x", x=P)).then_inc(ao_out[j], 16)

        turns(sp, step)
        store(NGRP - 1, NT - 1, HKV - 1, 1)
        for j in range(2):
            sp.wait_ge(ao_out[j], 16 * NGRP // 2)

    @block.gpsimd
    def _(pool):
        pool.memset(f32(VZ.hi[:]), 0.0).then_inc(zeroed, 1)
        pool.memset(f32(VZ.lo[:]), 0.0).then_inc(zeroed, 1)

        def rope_k(tt):
            pool.wait_ge(k_terms, 3 * tt + 3)
            wait(pool, t_mm, order_k(tt - 1) + 1)
            for dup in range(2):
                pool.tensor_tensor(KN[:, :, dup, :], KR[:, 0].rearrange("p (g x) -> p g x", x=DH),
                                   KR[:, 1].rearrange("p (g x) -> p g x", x=DH), ALU.add).then_inc(k_roped, 1)

        def rope_q(u, tt, g):
            pool.wait_ge(q_terms, 3 * u + 3)
            pool.wait_ge(t_mm, order_q(tt, g) - (1 if g else 2) + 1)
            pool.tensor_tensor(QN[:], QR[:, 0], QR[:, 1], ALU.add).then_inc(q_roped, 1)

        def norm(u, j):
            pool.wait_ge(recip_made, u + 1)
            for a in range(2):
                heads = slice(a * KC, (a + 1) * KC)
                pool.tensor_tensor(PR[j][:, heads, :], PR[j][:, heads, :],
                                   rinv[j][:, heads].unsqueeze(2).to_broadcast([P, KC, P]),
                                   ALU.mult).then_inc(normed, 1)

        rope_k(0)
        pool.wait_ge(q_terms, 3)
        pool.tensor_tensor(QN[:], QR[:, 0], QR[:, 1], ALU.add).then_inc(q_roped, 1)
        rope_q(1, 0, 1)
        norm(0, 0)

        def step(i, v, last):
            u, tt, g, ahead = plan(i, v, last)
            if ahead(2):
                if g == 2:
                    rope_k(tt + 1)
                rope_q(u + 2, tt + (g + 2) // HKV, (g + 2) % HKV)
            if ahead(1):
                norm(u + 1, (v + 1) % 2)

        turns(pool, step)

    @block.scalar
    def _(act):
        def high(c):
            act.wait_ge(w_in[c], 16)
            act.copy(W.hi[:, c], raw[c][:]).then_inc(w_hi, 1)

        def turned(order, dst):
            act.wait_ge(t_mm, order + 1)
            act.copy(dst[:].rearrange("p a x -> p (a x)"), psT[:]).then_inc(t_out, 1)

        def exps(u, j):
            act.wait_ge(max_made, u + 1)
            for h in range(REP):
                act.activation(PR[j][:, h, :], psS[:, h, :], ACT.Exp, bias=nmax[j][:, h:h + 1],
                               accum_out=rsum[j][:, h:h + 1]).then_inc(exp_done, 1)

        def v_high(tt):
            act.wait_ge(kv_mm, tt + 1)
            wait(act, pv_mm, HKV * tt)
            act.copy(VZ.hi[:, :, DH:2 * DH], psK[:, HKV * DH:].rearrange("p (g x) -> p g x", x=DH)).then_inc(v_hi, 1)

        def attn_out(u, i, v):
            act.wait_ge(pv_mm, u + 1)
            wait(act, ao_out[v % 2], 16 * (GI // 2 * i + v // 2))
            act.copy(AO[v % 2][:], psO[:]).then_inc(ao_made, 1)

        high(0)
        high(1)
        act.wait_ge(tab_in, 32)
        act.copy(mask[:], mask_f[:]).then_inc(consts, 1)
        act.copy(ident_r[:], ident[:]).then_inc(consts, 1)
        high(2)
        turned(order_k(0), KT)
        turned(order_q(0, 0), QT2[0])
        high(3)
        exps(0, 0)
        turned(order_q(0, 1), QT2[1])
        high(4)
        act.wait_ge(zeroed, 2)

        def step(i, v, last):
            u, tt, g, ahead = plan(i, v, last)
            for a in range(2):
                act.wait_ge(p_mm, 2 * u + a + 1)
                wait(act, pv_mm, u - 1)
                act.copy(PT[v % 2].hi[:, a * KC:(a + 1) * KC, :], psP[:, a * KC:(a + 1) * KC, :]).then_inc(p_hi, 1)
            if ahead(1):
                exps(u + 1, (v + 1) % 2)
            if ahead(2):
                if g == 2:
                    turned(order_k(tt + 1), KT)
                turned(order_q(tt + (g + 2) // HKV, (g + 2) % HKV), QT2[v % 2])
            if not (isinstance(u, int) and u == 0):
                attn_out(u - 1, i if v else i - 1, (v - 1) % GI)
            if g == 0:
                v_high(tt)

        turns(act, step)
        attn_out(NGRP - 1, NT // 2 - 1, GI - 1)

    @block.vector
    def _(dve):
        def terms(src, dst, rows, scaled, made):
            x, cs, sn = halves(src), halves(dst[:, 0]), halves(dst[:, 1])
            n = rows
            c = tab[:, scaled, 0, :].unsqueeze(1).to_broadcast([P, 2 * n, DH // 2])
            dve.tensor_tensor(cs.rearrange("p h two x -> p (h two) x"), x.rearrange("p h two x -> p (h two) x"),
                              c, ALU.mult).then_inc(made, 1)
            for a in range(2):
                s = tab[:, scaled, 1 + a, :].unsqueeze(1).to_broadcast([P, n, DH // 2])
                dve.tensor_tensor(sn[:, :, a, :], x[:, :, 1 - a, :], s, ALU.mult).then_inc(made, 1)

        def terms_k(tt):
            dve.wait_ge(kv_mm, tt + 1)
            wait(dve, k_roped, 2 * tt)
            terms(psK[:, 0:HKV * DH], KR, HKV, 1, k_terms)

        def terms_q(u):
            dve.wait_ge(q_mm, u + 1)
            wait(dve, q_roped, u)
            terms(psQ[:], QR, REP, 0, q_terms)

        def low(c):
            dve.wait_ge(w_hi, c + 1)
            dve.tensor_tensor(W.lo[:, c], raw[c][:], f32(W.hi[:, c]), ALU.subtract).then_inc(w_ready, 1)

        def maxes(u, j):
            dve.wait_ge(s_mm, u + 1)
            dve.tensor_reduce(nmax[j][:], psS[:], AX.X, ALU.max, negate=True).then_inc(max_made, 1)

        def recips(u, j):
            dve.wait_ge(exp_done, REP * (u + 1))
            dve.reciprocal(rinv[j][:], rsum[j][:]).then_inc(recip_made, 1)

        def v_low(tt):
            dve.wait_ge(v_hi, tt + 1)
            dve.tensor_tensor(VZ.lo[:, :, DH:2 * DH], psK[:, HKV * DH:].rearrange("p (g x) -> p g x", x=DH),
                              f32(VZ.hi[:, :, DH:2 * DH]), ALU.subtract).then_inc(v_lo, 1)

        low(0)
        low(1)
        dve.wait_ge(tab_in, 32)
        terms_k(0)
        terms_q(0)
        low(2)
        terms_q(1)
        low(3)
        maxes(0, 0)
        low(4)
        recips(0, 0)

        def step(i, v, last):
            u, tt, g, ahead = plan(i, v, last)
            if ahead(2):
                if g == 2:
                    terms_k(tt + 1)
                terms_q(u + 2)
            if ahead(1):
                maxes(u + 1, (v + 1) % 2)
            for a in range(2):
                heads = slice(a * KC, (a + 1) * KC)
                dve.wait_ge(p_hi, 2 * u + a + 1)
                dve.tensor_tensor(PT[v % 2].lo[:, heads, :], psP[:, heads, :], f32(PT[v % 2].hi[:, heads, :]),
                                  ALU.subtract).then_inc(p_lo, 1)
            if ahead(1):
                recips(u + 1, (v + 1) % 2)
            if g == 0:
                v_low(tt)

        turns(dve, step)

    @block.tensor
    def _(pe):
        def product(tt, j, n, c, out, made):
            pe.wait_ge(w_ready, c + 1)
            pe.wait_ge(ht_in[j], 16 * n)
            for k in range(KC):
                last = mm3(pe, out, (HT[j][:, 0, k, :], HT[j][:, 1, k, :]), W.at(ALL, c, k, ALL),
                           k == 0, k == KC - 1)
            last.then_inc(made, 1)

        def product_kv(tt, j, n):
            wait(pe, v_lo, tt)
            wait(pe, k_terms, 3 * tt)
            product(tt, j, n, 0, psK[:], kv_mm)

        def product_q(u, tt, j, n, g):
            wait(pe, q_terms, 3 * u)
            product(tt, j, n, 1 + g, psQ[:], q_mm)

        def turn(order, src, made, count):
            pe.wait_ge(made, count)
            wait(pe, t_out, order)
            for q in range(KC):
                last = pe.transpose(psT[:, q * P:(q + 1) * P], src[:, q * P:(q + 1) * P], ident[:])
            last.then_inc(t_mm, 1)

        def turn_k(tt):
            turn(order_k(tt), KN[:].rearrange("p g a x -> p (g a x)"), k_roped, 2 * tt + 2)

        def turn_q(u, tt, g):
            turn(order_q(tt, g), QN, q_roped, u + 1)

        def scores(u, tt, g, j):
            pe.wait_ge(t_out, order_q(tt, g) + 1)
            wait(pe, exp_done, REP * u)
            for a in range(2):
                pe.matmul(psS[:, a * KC:(a + 1) * KC, :], ident_r[:], mask[:], start=True, stop=False,
                          skip_group_check=True)
                rows = slice(a * DH, (a + 1) * DH)
                for h in range(KC):
                    last = pe.matmul(psS[:, a * KC + h, :], QT2[j][rows, h, :], KT[rows, g, :], start=False,
                                     stop=h == KC - 1, skip_group_check=True)
            last.then_inc(s_mm, 1)

        def turn_probs(u, j):
            pe.wait_ge(normed, 2 * u + 2)
            wait(pe, p_lo, 2 * u)
            for h in range(REP):
                last = pe.transpose(psP[:, h, :], PR[j][:, h, :], ident[:])
                if h % KC == KC - 1:
                    last.then_inc(p_mm, 1)

        def values(u, tt, g, j):
            pe.wait_ge(p_lo, 2 * u + 2)
            pe.wait_ge(v_lo, tt + 1)
            wait(pe, ao_made, u)
            for a in range(2):
                z = slice(DH, 3 * DH) if a == 0 else slice(0, 2 * DH)
                probs = PT[j].at(ALL, slice(a * KC, (a + 1) * KC), ALL)
                last = mm3(pe, psO[:], VZ.at(ALL, g, z), probs, a == 0, a == 1)
            last.then_inc(pv_mm, 1)

        product_kv(0, 0, 1)
        product_q(0, 0, 0, 1, 0)
        turn_k(0)
        turn_q(0, 0, 0)
        product_q(1, 0, 0, 1, 1)
        pe.wait_ge(consts, 2)
        scores(0, 0, 0, 0)
        turn_q(1, 0, 1)

        def step(i, v, last):
            u, tt, g, ahead = plan(i, v, last)
            t2, g2 = tt + (g + 2) // HKV, (g + 2) % HKV
            j2 = (v + 2) // HKV % 2
            n2 = i + 1 + (v + 2) // GI
            if ahead(2):
                if g == 2:
                    product_kv(t2, j2, n2)
                product_q(u + 2, t2, j2, n2, g2)
            if ahead(1):
                scores(u + 1, tt + (g + 1) // HKV, (g + 1) % HKV, (v + 1) % 2)
            turn_probs(u, v % 2)
            if not (isinstance(u, int) and u == 0):
                values(u - 1, tt if g else tt - 1, (g - 1) % HKV, (v - 1) % 2)
            if ahead(2):
                if g == 2:
                    turn_k(tt + 1)
                turn_q(u + 2, t2, g2)

        turns(pe, step)
        values(NGRP - 1, NT - 1, HKV - 1, 1)


def build_project(nc, ctx, sem, t, keep):
    ident, eps_pow, acc, h3T = keep["ident"], keep["eps_pow"], keep["acc"], keep["h3T"]
    nh = HQ // 2
    wc = 4

    def sb(name, shape, dt=F32):
        return ctx.enter_context(nc.sbuf_tensor(name, shape, dt))

    W = Pair(ctx, nc, "wo", [P, nh, D])
    raw = [sb(f"wo_raw{j}", [P, wc, D]) for j in range(2)]
    A = [sb(f"ao_tile{j}", [P, nh, P]) for j in range(2)]
    AS = [Pair(ctx, nc, f"ao_parts{j}", [P, nh, P]) for j in range(2)]
    X1 = [sb(f"x1_in{j}", [P, D]) for j in range(2)]
    HN = [sb(f"h3_tile{j}", [P, D]) for j in range(2)]
    st = [sb(f"st3_{j}", [P, 6]) for j in range(2)]
    mv = [sb(f"mv3_{j}", [P, 2]) for j in range(2)]
    var = [sb(f"var3_{j}", [P, 1]) for j in range(2)]
    rstd = [sb(f"rstd3_{j}", [P, 1]) for j in range(2)]
    psX = [ctx.enter_context(nc.psum_tensor(f"psX4_{j}", [P, BANK], F32)) for j in range(2)]
    psH = [ctx.enter_context(nc.psum_tensor(f"psH4_{j}", [P, BANK], F32)) for j in range(2)]

    w_in = [sem(f"wo_in{j}") for j in range(2)]
    a_in = [sem(f"a_in{j}") for j in range(2)]
    x_in = [sem(f"x1_in{j}") for j in range(2)]
    w_hi, w_ready = sem("wo_hi"), sem("wo_ready")
    a_hi, a_lo, proj, x2_made = sem("a_hi"), sem("a_lo"), sem("proj"), sem("x2_made")
    ln3, ln3_seen, rstd3, h3_made = sem("ln3"), sem("ln3_seen"), sem("rstd3"), sem("h3_made")
    h3_turned, h3_hi, h3_lo = sem("h3_turned"), sem("h3_hi"), sem("h3_lo")

    def tiles(eng, step):
        for j in range(2):
            step(j, j, 0, True)
        with eng.Fori(1, NT // 2 - 1) as i:
            for j in range(2):
                step(2 * i + j, j, i, True)
        for j in range(2):
            step(NT - 2 + j, j, NT // 2 - 1, j == 0)

    block = ctx.enter_context(nc.Block())

    @block.sync
    def _(sp):
        def load(tt, j):
            sp.dma_start(A[j][:], t["ao"][tt]).then_inc(a_in[j], 16)
            sp.dma_start(X1[j][:], t["x1"][tt]).then_inc(x_in[j], 16)

        def load_w(c):
            sp.dma_start(raw[c % 2][:], t["w_o"][:, c * wc:(c + 1) * wc, :]).then_inc(w_in[c % 2], 16)

        load_w(0)
        load(0, 0)
        load_w(1)
        for c in range(2, nh // wc):
            sp.wait_ge(w_ready, c - 1)
            load_w(c)
        load(1, 1)
        with sp.Fori(1, NT // 2) as i:
            for j in range(2):
                sp.wait_ge(a_lo, 2 * i + j - 1)
                sp.wait_ge(x2_made, 2 * i + j - 1)
                load(2 * i + j, j)

    @block.gpsimd
    def _(pool):
        def split(tt, j):
            pool.wait_ge(a_hi, tt + 1)
            pool.tensor_tensor(AS[j].lo[:], A[j][:], f32(AS[j].hi[:]), ALU.subtract).then_inc(a_lo, 1)

        def step(tt, j, i, more):
            if more:
                split(tt + 1, 1 - j)
            pool.wait_ge(ln3, 3 * tt + 3)
            pool.tensor_tensor(rstd[j][:], var[j][:], eps_pow[:], ALU.pow).then_inc(rstd3, 1)

        split(0, 0)
        tiles(pool, step)

    @block.scalar
    def _(act):
        def split(tt, j, n):
            act.wait_ge(a_in[j], 16 * n)
            wait(act, proj, tt - 1)
            act.copy(AS[j].hi[:], A[j][:]).then_inc(a_hi, 1)

        def turned(tt, j):
            act.wait_ge(h3_turned, tt + 1)
            act.copy(h3T.hi[:, :, bass.ds(tt * P, P)], psH[j][:].rearrange("p (k x) -> p k x", k=KC)).then_inc(h3_hi, 1)

        def step(tt, j, i, more):
            if more:
                split(tt + 1, 1 - j, i + 1 + j)
            if not (isinstance(tt, int) and tt == 0):
                turned(tt - 1, 1 - j)

        for c in range(nh // wc):
            act.wait_ge(w_in[c % 2], 16 * (c // 2 + 1))
            act.copy(W.hi[:, c * wc:(c + 1) * wc, :], raw[c % 2][:]).then_inc(w_hi, 1)
            if c == 0:
                split(0, 0, 1)
        tiles(act, step)
        turned(NT - 1, 1)

    @block.vector
    def _(dve):
        def turned(tt, j):
            dst = bass.ds(tt * P, P)
            dve.wait_ge(h3_hi, tt + 1)
            dve.tensor_tensor(h3T.lo[:, :, dst], psH[j][:].rearrange("p (k x) -> p k x", k=KC),
                              f32(h3T.hi[:, :, dst]), ALU.subtract).then_inc(h3_lo, 1)

        def step(tt, j, i, more):
            x2 = acc[:, bass.ds(tt, 1), :].rearrange("p o c -> p (o c)")
            dve.wait_ge(proj, tt + 1)
            dve.wait_ge(x_in[j], 16 * (i + 1))
            dve.tensor_tensor(x2, psX[j][:], X1[j][:], ALU.add).then_inc(x2_made, 1)
            dve.wait_ge(x2_made, tt + 1)
            dve.sem_inc(ln3_seen, 1)
            dve.bn_stats(st[j][:], x2).then_inc(ln3, 1)
            dve.wait_ge(ln3, 3 * tt + 1)
            dve.sem_inc(ln3_seen, 1)
            dve.bn_aggr(mv[j][:], st[j][:]).then_inc(ln3, 1)
            dve.wait_ge(ln3, 3 * tt + 2)
            dve.tensor_scalar(var[j][:], mv[j][:, 1:2], EPS, None, ALU.add).then_inc(ln3, 1)
            if not (isinstance(tt, int) and tt == 0):
                turned(tt - 1, 1 - j)
            dve.wait_ge(rstd3, tt + 1)
            dve.tensor_scalar(HN[j][:], x2, mv[j][:, 0:1], rstd[j][:], ALU.subtract, ALU.mult).then_inc(h3_made, 1)

        for c in range(nh // wc):
            dve.wait_ge(w_hi, c + 1)
            dst = slice(c * wc, (c + 1) * wc)
            dve.tensor_tensor(W.lo[:, dst, :], raw[c % 2][:], f32(W.hi[:, dst, :]), ALU.subtract).then_inc(w_ready, 1)
        tiles(dve, step)
        turned(NT - 1, 1)

    @block.tensor
    def _(pe):
        def turn(tt, j):
            pe.wait_ge(h3_made, tt + 1)
            wait(pe, h3_lo, tt - 1)
            for k in range(KC):
                last = pe.transpose(psH[j][:, k * P:(k + 1) * P], HN[j][:, k * P:(k + 1) * P], ident[:])
            last.then_inc(h3_turned, 1)

        def step(tt, j, i, more):
            pe.wait_ge(a_lo, tt + 1)
            wait(pe, x2_made, tt - 1)
            for h in range(nh):
                if h % wc == 0:
                    pe.wait_ge(w_ready, h // wc + 1)
                last = mm3(pe, psX[j][:], AS[j].at(ALL, h, ALL), W.at(ALL, h, ALL), h == 0, h == nh - 1)
            last.then_inc(proj, 1)
            if not (isinstance(tt, int) and tt == 0):
                turn(tt - 1, 1 - j)

        tiles(pe, step)
        turn(NT - 1, 1)


def build_experts(nc, ctx, sem, t, keep):
    acc, h3T = keep["acc"], keep["h3T"]
    w_gu = 2 * KC * I
    w_cols = w_gu + NIT * D
    ne = NE + 1

    def sb(name, shape, dt=F32):
        return ctx.enter_context(nc.sbuf_tensor(name, shape, dt))

    raw = [sb(f"wexp_raw{j}", [P, w_cols]) for j in range(2)]
    W = [Pair(ctx, nc, f"wexp{j}", [P, w_cols]) for j in range(2)]
    Hd = Pair(ctx, nc, "hidden", [P, NIT, T])
    SG = [sb(f"silu{j}", [P, BANK]) for j in range(2)]
    HF = [sb(f"hidden_f32_{j}", [P, BANK]) for j in range(2)]
    gate_f, gate = sb("gate_f", [P, KC, NE]), Pair(ctx, nc, "gate_w", [P, KC, NE])
    bias, tri, tri_g = sb("bias_rows", [P, NE]), sb("tri_rows", [P, NE, NE]), sb("tri_g_rows", [P, GS, GS])
    sig, V, wts = sb("scores", [P, NT, NE]), sb("biased", [P, NT, NE]), sb("weights", [P, NT, NE])
    rank, masked = sb("rank", [P, NT, NE]), sb("masked", [P, NT, NE])
    above, equal = sb("above", [P, NT, NE, NE]), sb("equal", [P, NT, NE, NE])
    gsum, grank, gmask, gpen = (sb(n, [P, NT, NG]) for n in ("gsum", "grank", "gmask", "gpen"))
    wsum = sb("wsum", [P, NT])
    cw = sb("expert_weight", [P, ne, NT])

    psA = [ctx.enter_context(nc.psum_tensor(f"psA{j}", [P, 2, BANK], F32)) for j in range(2)]
    psD = [ctx.enter_context(nc.psum_tensor(f"psD{j}", [P, BANK], F32)) for j in range(4)]
    logits = psD[0][:, 0:NT * NE].rearrange("p (t e) -> p t e", e=NE)

    w_in = [sem(f"wexp_in{j}") for j in range(2)]
    w_hi, w_lo = sem("wexp_hi"), sem("wexp_lo")
    route_in, gate_hi, gate_lo, logit_mm, sig_made = (
        sem(n) for n in ("route_in", "gate_hi", "gate_lo", "logit_mm", "sig_made"))
    route, ones_made, cw_made = sem("route"), sem("ones_made"), sem("cw_made")
    a_mm, silu_made, prod_made, hid_hi, hid_lo = (
        sem(n) for n in ("a_mm", "silu_made", "prod_made", "hid_hi", "hid_lo"))
    d_mm, acc_made, out_sem = sem("d_mm"), sem("acc_made"), sem("out_done")

    def experts(eng, step):
        for j in range(2):
            step(j, j, 0, True)
        with eng.Fori(1, ne // 2) as i:
            for j in range(2):
                step(2 * i + j, j, i, True)
        step(ne - 1, 0, ne // 2, False)

    M = 2 * NIT

    block = ctx.enter_context(nc.Block())

    @block.sync
    def _(sp):
        sp.dma_start(raw[0][:], t["w_exp"][0]).then_inc(w_in[0], 16)
        sp.dma_start(gate_f[:], t["gate_w"]).then_inc(route_in, 16)
        sp.dma_start(bias[:], t["bias"].to_broadcast([P, NE])).then_inc(route_in, 16)
        sp.dma_start(tri[:].rearrange("p i j -> p (i j)"), t["tri"].to_broadcast([P, NE * NE])).then_inc(route_in, 16)
        sp.dma_start(tri_g[:].rearrange("p i j -> p (i j)"), t["tri_g"].to_broadcast([P, GS * GS])).then_inc(route_in, 16)
        sp.dma_start(raw[1][:], t["w_exp"][1]).then_inc(w_in[1], 16)

        def load(e, j):
            sp.wait_ge(w_lo, e - 1)
            sp.dma_start(raw[j][:], t["w_exp"][e]).then_inc(w_in[j], 16)

        with sp.Fori(1, ne // 2) as i:
            for j in range(2):
                load(2 * i + j, j)
        load(ne - 1, 0)
        for tt in range(NT):
            sp.wait_ge(acc_made, NT * (ne - 1) + tt + 1)
            sp.dma_start(t["out"][tt], acc[:, tt, :]).then_inc(out_sem, 16)
        sp.wait_ge(out_sem, 16 * NT)

    @block.gpsimd
    def _(pool):
        def split(e, j):
            pool.wait_ge(w_hi, e + 1)
            pool.tensor_tensor(W[j].lo[:], raw[j][:], f32(W[j].hi[:]), ALU.subtract).then_inc(w_lo, 1)

        pool.memset(cw[:, 0, :], 1.0).then_inc(ones_made, 1)
        split(0, 0)

        def step(e, j, i, more):
            if more:
                split(e + 1, 1 - j)
            for m in range(M):
                it, cols = m % NIT, slice(m // NIT * BANK, (m // NIT + 1) * BANK)
                pool.wait_ge(hid_hi, M * e + m + 1)
                pool.tensor_tensor(Hd.lo[:, it, cols], HF[m % 2][:], f32(Hd.hi[:, it, cols]),
                                   ALU.subtract).then_inc(hid_lo, 1)

        experts(pool, step)

    @block.scalar
    def _(act):
        def split(e, j, n):
            act.wait_ge(w_in[j], 16 * n)
            wait(act, d_mm, NT * (e - 1))
            act.copy(W[j].hi[:], raw[j][:]).then_inc(w_hi, 1)

        act.wait_ge(route_in, 64)
        act.copy(gate.hi[:], gate_f[:]).then_inc(gate_hi, 1)
        split(0, 0, 1)
        act.wait_ge(logit_mm, 1)
        act.activation(sig[:], logits, ACT.Sigmoid).then_inc(sig_made, 1)

        def step(e, j, i, more):
            if more:
                split(e + 1, 1 - j, i + 1 + j)
            for m in range(M):
                act.wait_ge(a_mm, M * e + m + 1)
                wait(act, prod_made, M * e + m - 1)
                act.activation(SG[m % 2][:], psA[m % 2][:, 0, :], ACT.Silu).then_inc(silu_made, 1)
                act.wait_ge(prod_made, M * e + m + 1)
                wait(act, d_mm, NT * e)
                cols = slice(m // NIT * BANK, (m // NIT + 1) * BANK)
                act.copy(Hd.hi[:, m % NIT, cols], HF[m % 2][:]).then_inc(hid_hi, 1)

        experts(act, step)

    @block.vector
    def _(dve):
        route_count = [0]

        def link(ins):
            route_count[0] += 1
            ins.then_inc(route, 1)
            dve.wait_ge(route, route_count[0])

        def ranks(values, n, size, tri_m, ab, eq, out):
            vj = values.unsqueeze(2).to_broadcast([P, n, size, size])
            vi = values.unsqueeze(3).to_broadcast([P, n, size, size])
            low = tri_m.unsqueeze(1).to_broadcast([P, n, size, size])
            dve.tensor_tensor(ab, vj, vi, ALU.is_gt).then_inc(route, 1)
            route_count[0] += 1
            link(dve.tensor_tensor(eq, vj, vi, ALU.is_equal))
            link(dve.tensor_tensor(eq, eq, low, ALU.mult))
            link(dve.tensor_tensor(ab, ab, eq, ALU.add))
            link(dve.tensor_reduce(out, ab, AX.X, ALU.add))

        def by_group(ap):
            return ap.rearrange("p t (g x) -> p (t g) x", x=GS)

        def small(ap, n, size):
            return ap[:].rearrange("p t i j -> p (t i j)")[:, 0:n * size * size].rearrange(
                "p (n i j) -> p n i j", i=size, j=size)

        def route_groups():
            dve.wait_ge(sig_made, 1)
            dve.wait_ge(route_in, 64)
            link(dve.tensor_tensor(V[:], sig[:], bias[:].unsqueeze(1).to_broadcast([P, NT, NE]), ALU.add))
            ranks(by_group(V[:]), NT * NG, GS, tri_g[:], small(above, NT * NG, GS), small(equal, NT * NG, GS),
                  by_group(rank[:]))
            link(dve.scalar_tensor_tensor(masked[:], rank[:], 2.0, V[:], ALU.is_lt, ALU.mult))
            link(dve.tensor_reduce(gsum[:].rearrange("p t g -> p (t g)"), by_group(masked[:]), AX.X, ALU.add))
            ranks(gsum[:], NT, NG, tri_g[:], small(above, NT, NG), small(equal, NT, NG), grank[:])
            link(dve.tensor_scalar(gmask[:], grank[:], float(TOPG), None, ALU.is_lt))
            link(dve.tensor_scalar(gpen[:], gmask[:], 1.0, 1e30, ALU.subtract, ALU.mult))

        def route_mask():
            wide = lambda ap: ap[:].rearrange("p t g -> p (t g)").unsqueeze(2).to_broadcast([P, NT * NG, GS])
            link(dve.tensor_tensor(by_group(masked[:]), by_group(V[:]), wide(gmask), ALU.mult))
            link(dve.tensor_tensor(by_group(masked[:]), by_group(masked[:]), wide(gpen), ALU.add))

        def route_experts():
            ranks(masked[:], NT, NE, tri[:], above[:], equal[:], rank[:])

        def route_weights():
            link(dve.scalar_tensor_tensor(wts[:], rank[:], float(TOPK), sig[:], ALU.is_lt, ALU.mult))
            link(dve.tensor_reduce(wsum[:], wts[:], AX.X, ALU.add))
            link(dve.tensor_scalar(wsum[:], wsum[:], 1e-20, None, ALU.add))
            link(dve.reciprocal(wsum[:], wsum[:]))
            link(dve.tensor_tensor(wts[:], wts[:], wsum[:].unsqueeze(2).to_broadcast([P, NT, NE]), ALU.mult))
            dve.tensor_scalar(cw[:, 1:, :].rearrange("p e t -> p t e"), wts[:], SCALING, None,
                              ALU.mult).then_inc(cw_made, 1)

        dve.wait_ge(gate_hi, 1)
        dve.tensor_tensor(gate.lo[:], gate_f[:], f32(gate.hi[:]), ALU.subtract).then_inc(gate_lo, 1)

        def step(e, j, i, more):
            first = isinstance(e, int) and e == 0
            for m in range(M):
                dve.wait_ge(silu_made, M * e + m + 1)
                wait(dve, hid_lo, M * e + m - 1)
                dve.tensor_tensor(HF[m % 2][:], psA[m % 2][:, 1, :], SG[m % 2][:], ALU.mult).then_inc(prod_made, 1)
                if first:
                    (route_groups, route_mask, route_experts, route_weights)[m]()
            if first:
                dve.wait_ge(ones_made, 1)
            elif isinstance(e, int) and e == 1:
                dve.wait_ge(cw_made, 1)
            for tt in range(NT):
                dve.wait_ge(d_mm, NT * e + tt + 1)
                wait(dve, acc_made, NT * e - NT + tt + 1)
                dve.scalar_tensor_tensor(acc[:, tt, :], psD[tt % 4][:],
                                         cw[:, bass.ds(e, 1), tt:tt + 1].rearrange("p o t -> p (o t)"),
                                         acc[:, tt, :], ALU.mult, ALU.add).then_inc(acc_made, 1)

        experts(dve, step)

    @block.tensor
    def _(pe):
        pe.wait_ge(gate_lo, 1)
        for tt in range(NT):
            for k in range(KC):
                last = mm3(pe, logits[:, tt, :], h3T.at(ALL, k, slice(tt * P, (tt + 1) * P)),
                           gate.at(ALL, k, ALL), k == 0, k == KC - 1)
        last.then_inc(logit_mm, 1)

        def step(e, j, i, more):
            pe.wait_ge(w_lo, e + 1)
            w = W[j]
            for m in range(M):
                it, cols = m % NIT, slice(m // NIT * BANK, (m // NIT + 1) * BANK)
                wait(pe, prod_made, M * e + m - 1)
                for a in range(2):
                    for k in range(KC):
                        at = (a * KC + k) * I + it * P
                        last = mm3(pe, psA[m % 2][:, a, :], w.at(ALL, slice(at, at + P)), h3T.at(ALL, k, cols),
                                   k == 0, k == KC - 1)
                last.then_inc(a_mm, 1)
            for tt in range(NT):
                if tt % (NT // 2) == 0:
                    pe.wait_ge(hid_lo, M * e + (tt // (NT // 2) + 1) * NIT)
                wait(pe, acc_made, NT * e + tt - 3)
                if isinstance(e, int) and e == 0 and tt == 0:
                    pe.wait_ge(sig_made, 1)
                for k in range(NIT):
                    last = mm3(pe, psD[tt % 4][:], Hd.at(ALL, k, slice(tt * P, (tt + 1) * P)),
                               w.at(ALL, slice(w_gu + k * D, w_gu + (k + 1) * D)), k == 0, k == NIT - 1)
                last.then_inc(d_mm, 1)

        experts(pe, step)



def build(nc, t):
    outer = ExitStack()
    with outer:
        made = []

        def sem(name):
            made.append(name)
            return outer.enter_context(nc.semaphore(name))

        ident = outer.enter_context(nc.sbuf_tensor("ident", [P, P], F32))
        eps_pow = outer.enter_context(nc.sbuf_tensor("eps_pow", [P, 1], F32))
        keep = {"ident": ident, "eps_pow": eps_pow}
        with ExitStack() as attn:
            keep["F"] = Pair(attn, nc, "F", [P, H, D])
            with ExitStack() as ctx:
                keep["h1T"] = Pair(ctx, nc, "h1T", [P, KC, T])
                build_queries(nc, ctx, sem, t["x"], t["w_pairs"], t["qe"], keep)
            with ExitStack() as ctx:
                build_cross(nc, ctx, sem, t, keep)
        with ExitStack() as ctx:
            build_self(nc, ctx, sem, t, keep)
        with ExitStack() as rest:
            keep["acc"] = rest.enter_context(nc.sbuf_tensor("acc", [P, NT, D], F32))
            keep["h3T"] = Pair(rest, nc, "h3T", [P, KC, T])
            with ExitStack() as ctx:
                build_project(nc, ctx, sem, t, keep)
            with ExitStack() as ctx:
                build_experts(nc, ctx, sem, t, keep)


def _pack_pairs(w_kc_q, W_qr, Wq, W_kr, w_kc_kv, Wo):
    kq = w_kc_q.reshape(NP, 2, P, QT, P).transpose(0, 4, 1, 3, 2).reshape(NP, P, W_KQ)
    qr = W_qr.reshape(NP, 2, QT, P, R).transpose(0, 3, 1, 2, 4).reshape(NP, P, W_QR)
    wq = Wq.reshape(NP, 2, P, D).transpose(0, 2, 1, 3).reshape(NP, P, W_Q)
    kr = W_kr.transpose(0, 2, 1).reshape(NP, P, P)
    kv = w_kc_kv.reshape(NP, 2, P, DC).transpose(0, 2, 1, 3).reshape(NP, P, W_KV)
    wo = Wo.T.reshape(NP, 2, P, D).transpose(0, 2, 1, 3).reshape(NP, P, W_O)
    return np.concatenate([kq, qr, wq, kr, kv, wo], axis=2)


def _rope_cross():
    inv = (1.0 / 10000.0 ** (np.arange(0, DC, 2, dtype=np.float32) / np.float32(DC))).astype(np.float32)
    freqs = (np.arange(L, dtype=np.float32)[:, None] * inv[None, :]).astype(np.float32)
    sign = np.where(np.arange(DC // 2) < DC // 4, -1.0, 1.0).astype(np.float32)
    return np.stack([np.cos(freqs), np.sin(freqs) * sign], 1).reshape(P, LT, 2, DC // 2).transpose(0, 2, 1, 3)


def _rope_self():
    inv = (1.0 / 10000.0 ** (np.arange(0, DH, 2, dtype=np.float32) / np.float32(DH))).astype(np.float32)
    ang = ((np.arange(P) % S).astype(np.float32)[:, None] * inv[None, :]).astype(np.float32)
    k = np.stack([np.cos(ang), -np.sin(ang), np.sin(ang)], 1)
    return np.stack([k * np.float32(DH ** -0.5), k], 1).astype(np.float32)


def _mask_self():
    r, c = np.arange(P)[:, None], np.arange(P)[None, :]
    m = np.where((r // S == c // S) & (c <= r), 0.0, -1e30).astype(np.float32)
    return np.tile(m, (1, BANK // P))


def _rows(w):
    return w.T.reshape(w.shape[1] // P, P, w.shape[0]).transpose(1, 0, 2)


def kernel(x, ctx_512, L0_xattn_Wq, L0_xattn_w_kc_q, L0_xattn_w_kc_kv, L0_xattn_W_qr, L0_xattn_W_kr,
           L0_xattn_Wo, L0_attn_w_qkv, L0_attn_w_o, L0_ffn_gate_weight, L0_ffn_expert_bias,
           L0_ffn_gate_proj, L0_ffn_up_proj, L0_ffn_down_proj, L0_ffn_shared_gate, L0_ffn_shared_up,
           L0_ffn_shared_down):
    import concourse.bacc as bacc
    from concourse.bass_utils import run_bass_kernel_spmd as run

    A = np.asarray
    w_qkv = A(L0_attn_w_qkv)
    nq = HQ * DH
    wkv_first = np.concatenate([w_qkv[nq:], w_qkv[:nq]], axis=0)
    gates = np.concatenate([A(L0_ffn_shared_gate)[None], A(L0_ffn_gate_proj)])
    ups = np.concatenate([A(L0_ffn_shared_up)[None], A(L0_ffn_up_proj)])
    downs = np.concatenate([A(L0_ffn_shared_down)[None], A(L0_ffn_down_proj)])
    gu = np.stack([gates, ups], 1).reshape(NE + 1, 2, I, KC, P).transpose(0, 4, 1, 3, 2)
    dn = downs.reshape(NE + 1, D, NIT, P).transpose(0, 3, 2, 1)
    arrays = {
        "x": A(x).reshape(NT, P, D),
        "ctx": A(ctx_512).reshape(B, P, LT * DC),
        "w_pairs": _pack_pairs(A(L0_xattn_w_kc_q), A(L0_xattn_W_qr), A(L0_xattn_Wq), A(L0_xattn_W_kr),
                               A(L0_xattn_w_kc_kv), A(L0_xattn_Wo)),
        "rope_x": _rope_cross().reshape(P, 2, LT * DC // 2),
        "w_qkv": _rows(wkv_first).reshape(P, KC, 5, BANK).transpose(2, 0, 1, 3),
        "rope_s": _rope_self(),
        "mask": _mask_self(),
        "w_o": _rows(A(L0_attn_w_o)),
        "gate_w": _rows(A(L0_ffn_gate_weight)),
        "bias": A(L0_ffn_expert_bias).reshape(1, NE),
        "tri": (np.arange(NE)[None, :] < np.arange(NE)[:, None]).astype(np.float32).reshape(1, NE * NE),
        "tri_g": (np.arange(GS)[None, :] < np.arange(GS)[:, None]).astype(np.float32).reshape(1, GS * GS),
        "w_exp": np.concatenate([gu.reshape(NE + 1, P, 2 * KC * I), dn.reshape(NE + 1, P, NIT * D)], 2),
    }
    arrays = {n: np.ascontiguousarray(a) for n, a in arrays.items()}
    nc = bacc.Bacc("TRN2", target_bir_lowering=False, num_devices=1)
    t = {n: nc.dram_tensor(n, a.shape, F32, kind="ExternalInput").ap() for n, a in arrays.items()}
    t["out"] = nc.dram_tensor("out", (NT, P, D), F32, kind="ExternalOutput").ap()
    t["qe"] = nc.dram_tensor("qe", (2, B, P, NP, 2 * S), F32).ap()
    t["x1"] = nc.dram_tensor("x1", (NT, P, D), F32).ap()
    t["h2T"] = nc.dram_tensor("h2T", (NT, P, 2, D), F32).ap()
    t["ao"] = nc.dram_tensor("ao", (NT, P, HQ // 2, P), F32).ap()
    build(nc, t)
    r = run(nc, [arrays], core_ids=[0])
    return r.results[0]["out"].reshape(B, S, D)
```

```python
from contextlib import ExitStack

import numpy as np

import concourse.bass as bass
from concourse import mybir

F32 = mybir.dt.float32
F32R = mybir.dt.float32r
ALU = mybir.AluOpType
ACT = mybir.ActivationFunctionType
AX = mybir.AxisListType

P = 128
B, S, D = 16, 64, 512
T = B * S
NT = T // P
KC = D // P
EPS = 1e-5
BANK = 512

L, DC, H, R, CQ = 1024, 128, 16, 64, 384
NP = H // 2
QT = CQ // P
LT = L // P
W_KQ, W_QR, W_Q = 2 * QT * P, 2 * QT * R, 2 * D
W_KR, W_KV, W_O = P, 2 * DC, 2 * D
W_A = W_KQ + W_QR + W_Q
W_B = W_KR + W_KV + W_O

HQ, HKV, DH = 32, 4, 64
REP = HQ // HKV

W_AHEAD = HQ * DH // P // KC

NE, TOPK, NG, TOPG, I = 16, 4, 4, 2, 256
GS = NE // NG
SCALING = 2.5
NIT = I // P


def mm3(pe, out, lhs, rhs, start, stop):
    pe.matmul(out, lhs[0], rhs[0], start=start, stop=False, skip_group_check=True)
    pe.matmul(out, lhs[0], rhs[1], start=False, stop=False, skip_group_check=True)
    return pe.matmul(out, lhs[1], rhs[0], start=False, stop=stop, skip_group_check=True)


class Pair:

    def __init__(self, ctx, nc, name, shape):
        self.hi = ctx.enter_context(nc.sbuf_tensor(name + "_hi", shape, F32R))
        self.lo = ctx.enter_context(nc.sbuf_tensor(name + "_lo", shape, F32R))

    def at(self, *idx):
        return self.hi[idx], self.lo[idx]


def f32(ap):
    return ap.bitcast(F32)


ALL = slice(None)


def rope_kv(pool, keep, b):
    kv, kr, kt, tab = keep["kv_raw"], keep["kv_rope"], keep["kv_term"], keep["rope_tab"]
    pair = lambda ap: ap.rearrange("p (a two) -> p a two", two=2)
    pool.wait_ge(keep["kv_in"], 16 * b + 16)
    pool.wait_ge(keep["rope_done"], b + 1)
    cos = tab[:, 0, :].unsqueeze(2).to_broadcast([P, LT * DC // 2, 2])
    pool.tensor_tensor(pair(kr), pair(kv), cos, ALU.mult).then_inc(keep["rope_part"], 1)
    quarter = DC // 4
    for half in range(2):
        dst = kt.rearrange("p (l h a two) -> p l h a two", h=2, a=quarter, two=2)[:, :, half]
        src = kv.rearrange("p (l h a two) -> p l h a two", h=2, a=quarter, two=2)[:, :, 1 - half]
        sin = tab[:, 1, :].rearrange("p (l h a) -> p l h a", h=2, a=quarter)[:, :, half, :]
        pool.tensor_tensor(dst, src, sin.unsqueeze(3).to_broadcast([P, LT, quarter, 2]),
                           ALU.mult).then_inc(keep["rope_part"], 1)
    pool.wait_ge(keep["rope_part"], 3 * b + 3)
    pool.tensor_tensor(kr, kr, kt, ALU.add).then_inc(keep["rope_done"], 1)


def build_queries(nc, ctx, sem, t, keep):
    x_d, w_pairs, qe_d = t["x"], t["w_pairs"], t["qe"]
    ident, F, h1T, eps_pow = keep["ident"], keep["F"], keep["h1T"], keep["eps_pow"]

    def sb(name, shape, dt=F32):
        return ctx.enter_context(nc.sbuf_tensor(name, shape, dt))

    XP = 4
    T_AT, C_AT = 4, 6
    raw = [sb(f"wraw{j}", [P, W_A + W_B]) for j in range(2)]
    WB = [Pair(ctx, nc, f"wb{j}", [P, W_B]) for j in range(2)]
    TW = sb("tw", [P, 2, R])
    C = Pair(ctx, nc, "cfold", [P, KC, P])
    Q = Pair(ctx, nc, "qr", [P, T])
    stage = sb("stage", [P, 2, T * 2])
    x_all = stage[:, :, :].rearrange("p a (b c) -> p (a b) c", c=D)
    stage_o = stage[:, :, :].rearrange("p a (b x) -> p a b x", b=B)
    stage_w = stage[:, :, :].bitcast(F32R).rearrange("p a (b j s) -> p a b j s", b=B, j=2)
    st = sb("st1", [P, NT, 6])
    mv = sb("mv1", [P, NT, 2])
    var = sb("var1", [P, NT])
    rstd = sb("rstd1", [P, NT])
    h = [sb(f"h1_{j}", [P, D]) for j in range(2)]

    psQ = ctx.enter_context(nc.psum_tensor("psQ", [P, 2, BANK], F32))
    psE = ctx.enter_context(nc.psum_tensor("psE", [P, 2, BANK], F32))
    psF = ctx.enter_context(nc.psum_tensor("psF", [P, 2, BANK], F32))
    psT = ctx.enter_context(nc.psum_tensor("psT", [P, BANK], F32))
    psC = ctx.enter_context(nc.psum_tensor("psC", [P, BANK], F32))

    x_in = [sem(f"x_in{a}") for a in range(XP)]
    w_in = [sem(f"w_in{j}") for j in range(2)]
    const_set, ln1, rstd1, h1_made = sem("const_set"), sem("ln1"), sem("rstd1"), sem("h1_made")
    h1_turned, h1_hi, h1_lo = sem("h1_turned"), sem("h1_hi"), sem("h1_lo")
    wB_hi, wB_ready = sem("wB_hi"), sem("wB_ready")
    t_mm, t_ready = sem("t_mm"), sem("t_ready")
    c_mm, c_hi, c_ready = sem("c_mm"), sem("c_hi"), sem("c_ready")
    q_mm, q_hi, q_ready = sem("q_mm"), sem("q_hi"), sem("q_ready")
    e_mm, e_hi, e_free = sem("e_mm"), sem("e_hi"), sem("e_free")
    f_mm, f_hi, f_free = sem("f_mm"), sem("f_hi"), sem("f_free")
    stage_out = sem("stage_out")

    def kq(w, j, qt):
        return w[:, (j * QT + qt) * P:(j * QT + qt + 1) * P]

    def qrw(w, j, qt):
        return w[:, W_KQ + (j * QT + qt) * R:W_KQ + (j * QT + qt + 1) * R]

    def wq(w, j, c):
        at = W_KQ + W_QR + j * D + c * P
        return w[:, at:at + P]

    block = ctx.enter_context(nc.Block())

    @block.sync
    def _(sp):
        for a in range(XP):
            part = slice(a * NT // XP, (a + 1) * NT // XP)
            sp.dma_start(x_all[:, part, :], x_d[part].rearrange("t p c -> p t c")).then_inc(x_in[a], 16)
        for j in range(2):
            sp.dma_start(raw[j][:], w_pairs[j]).then_inc(w_in[j], 16)
        sp.dma_start(keep["rope_tab"], t["rope_x"]).then_inc(keep["tab_in"], 16)
        sp.dma_start(keep["kv_raw"], t["ctx"][0]).then_inc(keep["kv_in"], 16)
        sp.sem_inc(stage_out, 32)

        def step(p, j, more):
            if more:
                sp.wait_ge(c_mm, p + 1)
                sp.wait_ge(wB_ready, p + 1)
                sp.dma_start(raw[j][:], w_pairs[p + 2]).then_inc(w_in[j], 16)
            sp.wait_ge(e_free, 4 * p + 4 + 2)
            for a in range(2):
                sp.dma_start(qe_d[a, :, :, p, :].rearrange("b d x -> d b x"),
                             stage_o[:, a]).then_inc(stage_out, 16)

        with sp.Fori(0, NP // 2 - 1) as i:
            for j in range(2):
                step(2 * i + j, j, True)
        for j in range(2):
            step(NP - 2 + j, j, False)
        sp.wait_ge(stage_out, 32 * (NP + 1))

    @block.gpsimd
    def _(pool):
        pool.memset(ident[:], 0.0).then_inc(const_set, 1)
        pool.memset(eps_pow[:], -0.5).then_inc(const_set, 1)
        pool.wait_ge(const_set, 2)
        pool.affine_select(out=ident[:], in_=ident[:], compare_op=ALU.not_equal, fill=1.0, base=0,
                           pattern=[[-1, P]], channel_multiplier=1).then_inc(const_set, 1)
        pool.wait_ge(ln1, NT + NT + 1)
        pool.tensor_tensor(rstd[:], var[:], eps_pow[:, 0:1].to_broadcast([P, NT]),
                           ALU.pow).then_inc(rstd1, 1)

        def split_low(j, q):
            pool.wait_ge(wB_hi, q + 1)
            pool.tensor_tensor(WB[j].lo[:], raw[j][:, W_A:], f32(WB[j].hi[:]), ALU.subtract).then_inc(wB_ready, 1)

        with pool.Fori(0, NP // 2) as i:
            for j in range(2):
                split_low(j, 2 * i + j)
        pool.sem_inc(keep["rope_done"], 1)
        pool.wait_ge(keep["tab_in"], 16)
        rope_kv(pool, keep, 0)

    @block.scalar
    def _(act):
        def split_high(j, n):
            act.wait_ge(w_in[j], 16 * n)
            act.copy(WB[j].hi[:], raw[j][:, W_A:]).then_inc(wB_hi, 1)

        def fold_t(q):
            act.wait_ge(t_mm, q + 1)
            act.copy(TW[:].rearrange("p j r -> p (j r)"), psT[:, 0:2 * R]).then_inc(t_ready, 1)

        def fold_c(q):
            act.wait_ge(c_mm, q + 1)
            act.copy(C.hi[:].rearrange("p k m -> p (k m)"), psC[:]).then_inc(c_hi, 1)

        for tt in range(NT):
            act.wait_ge(h1_turned, tt + 1)
            act.copy(h1T.hi[:, :, tt * P:(tt + 1) * P],
                     (psE if tt % 2 else psQ)[:, 0, :].rearrange("p (k t) -> p k t", k=KC)).then_inc(h1_hi, 1)
            if tt == T_AT:
                fold_t(0)
            if tt == C_AT:
                fold_c(0)
        split_high(0, 1)
        split_high(1, 1)

        def step(p, j, ahead, ahead2, n):
            for half in range(2):
                act.wait_ge(q_mm, 2 * p + half + 1)
                act.copy(Q.hi[:, half * BANK:(half + 1) * BANK], psQ[:, half]).then_inc(q_hi, 1)
            if ahead:
                fold_t(p + 1)
            act.wait_ge(stage_out, 32 * p + 32)
            for jj in range(2):
                for half in range(2):
                    act.wait_ge(e_mm, 4 * p + 2 * jj + half + 1)
                    act.copy(stage_w[:, 0, half * B // 2:(half + 1) * B // 2, jj, :],
                             psE[:, half].rearrange("p (b s) -> p b s", s=S)).then_inc(e_hi, 1)
                if ahead and jj == 0:
                    fold_c(p + 1)
            for jj in range(2):
                act.wait_ge(f_mm, 2 * p + jj + 1)
                act.copy(F.hi[:, bass.ds(2 * p + jj, 1), :], psF[:, jj:jj + 1]).then_inc(f_hi, 1)
            if ahead2:
                split_high(j, n)

        with act.Fori(0, NP // 2 - 1) as i:
            for j in range(2):
                step(2 * i + j, j, True, True, i + 2)
        step(NP - 2, 0, True, False, 0)
        step(NP - 1, 1, False, False, 0)

    @block.vector
    def _(dve):
        dve.sem_inc(e_free, 2)
        dve.sem_inc(f_free, 2)
        for tt in range(NT):
            dve.wait_ge(x_in[tt * XP // NT], 16)
            dve.bn_stats(st[:, tt, :], x_all[:, tt, :]).then_inc(ln1, 1)
            dve.wait_ge(ln1, 2 * tt + 1)
            dve.bn_aggr(mv[:, tt, :], st[:, tt, :]).then_inc(ln1, 1)
        dve.wait_ge(ln1, 2 * NT)
        dve.tensor_scalar(var[:], mv[:, :, 1], EPS, None, ALU.add).then_inc(ln1, 1)

        def norm(tt):
            if tt >= 2:
                dve.wait_ge(h1_turned, tt - 1)
            dve.tensor_scalar(h[tt % 2][:], x_all[:, tt, :], mv[:, tt, 0:1], rstd[:, tt:tt + 1],
                              ALU.subtract, ALU.mult).then_inc(h1_made, 1)

        def fold_c(q):
            dve.wait_ge(c_hi, q + 1)
            dve.tensor_tensor(C.lo[:].rearrange("p k m -> p (k m)"), psC[:],
                              f32(C.hi[:].rearrange("p k m -> p (k m)")), ALU.subtract).then_inc(c_ready, 1)

        dve.wait_ge(rstd1, 1)
        for tt in range(2):
            norm(tt)
        for tt in range(NT):
            dve.wait_ge(h1_hi, tt + 1)
            dst = slice(tt * P, (tt + 1) * P)
            dve.tensor_tensor(h1T.lo[:, :, dst], (psE if tt % 2 else psQ)[:, 0, :].rearrange("p (k t) -> p k t", k=KC),
                              f32(h1T.hi[:, :, dst]), ALU.subtract).then_inc(h1_lo, 1)
            if tt + 2 < NT:
                norm(tt + 2)
            if tt == C_AT:
                fold_c(0)

        def step(p, ahead):
            for half in range(2):
                cols = slice(half * BANK, (half + 1) * BANK)
                dve.wait_ge(q_hi, 2 * p + half + 1)
                dve.tensor_tensor(Q.lo[:, cols], psQ[:, half], f32(Q.hi[:, cols]),
                                  ALU.subtract).then_inc(q_ready, 1)
            for jj in range(2):
                for half in range(2):
                    bs = slice(half * B // 2, (half + 1) * B // 2)
                    dve.wait_ge(e_hi, 4 * p + 2 * jj + half + 1)
                    dve.tensor_tensor(stage_w[:, 1, bs, jj, :], psE[:, half].rearrange("p (b s) -> p b s", s=S),
                                      f32(stage_w[:, 0, bs, jj, :]), ALU.subtract).then_inc(e_free, 1)
                if ahead and jj == 0:
                    fold_c(p + 1)
            for jj in range(2):
                dve.wait_ge(f_hi, 2 * p + jj + 1)
                dst = bass.ds(2 * p + jj, 1)
                dve.tensor_tensor(F.lo[:, dst, :], psF[:, jj:jj + 1], f32(F.hi[:, dst, :]),
                                  ALU.subtract).then_inc(f_free, 1)

        with dve.Fori(0, NP // 2 - 1) as i:
            for j in range(2):
                step(2 * i + j, True)
        step(NP - 2, True)
        step(NP - 1, False)

    @block.tensor
    def _(pe):
        pe.wait_ge(const_set, 3)
        def fold_t(j, n):
            pe.wait_ge(w_in[j], 16 * n)
            for jj in range(2):
                for qt in range(QT):
                    last = pe.matmul(psT[:, jj * R:(jj + 1) * R], kq(raw[j], jj, qt), qrw(raw[j], jj, qt),
                                     start=qt == 0, stop=qt == QT - 1, skip_group_check=True)
            last.then_inc(t_mm, 1)

        def fold_c(q, j):
            pe.wait_ge(t_ready, q + 1)
            for c in range(KC):
                for jj in range(2):
                    at = c * P + jj * R
                    last = pe.matmul(psC[:, at:at + R], wq(raw[j], jj, c), TW[:, jj, :], start=True, stop=True,
                                     skip_group_check=True)
            last.then_inc(c_mm, 1)

        for tt in range(NT):
            pe.wait_ge(h1_made, tt + 1)
            if tt >= 2:
                pe.wait_ge(h1_lo, tt - 1)
            for k in range(KC):
                last = pe.transpose((psE if tt % 2 else psQ)[:, 0, k * P:(k + 1) * P],
                                    h[tt % 2][:, k * P:(k + 1) * P], ident[:])
            last.then_inc(h1_turned, 1)
            if tt == T_AT:
                fold_t(0, 1)
            if tt == C_AT:
                fold_c(0, 0)
        pe.wait_ge(h1_lo, NT)

        def step(p, j, ahead, n):
            pe.wait_ge(c_ready, p + 1)
            for half in range(2):
                for k in range(KC):
                    last = mm3(pe, psQ[:, half], C.at(ALL, k, ALL),
                               h1T.at(ALL, k, slice(half * BANK, (half + 1) * BANK)), k == 0, k == KC - 1)
                last.then_inc(q_mm, 1)
            if ahead:
                fold_t(1 - j, n)
            pe.wait_ge(wB_ready, p + 1)
            for jj in range(2):
                rows = slice(jj * R, (jj + 1) * R)
                for half in range(2):
                    pe.wait_ge(q_ready, 2 * p + half + 1)
                    pe.wait_ge(e_free, 4 * p + 2 * jj + half + 1)
                    mm3(pe, psE[:, half], WB[j].at(rows, slice(0, W_KR)),
                        Q.at(rows, slice(half * BANK, (half + 1) * BANK)), True, True).then_inc(e_mm, 1)
                if ahead and jj == 0:
                    fold_c(p + 1, 1 - j)
            for jj in range(2):
                pe.wait_ge(f_free, 2 * p + jj + 1)
                kv, wo = W_KR + jj * DC, W_KR + W_KV + jj * D
                mm3(pe, psF[:, jj], WB[j].at(ALL, slice(kv, kv + DC)), WB[j].at(ALL, slice(wo, wo + D)),
                    True, True).then_inc(f_mm, 1)

        with pe.Fori(0, NP // 2 - 1) as i:
            for j in range(2):
                step(2 * i + j, j, True, i + 1 + j)
        step(NP - 2, 0, True, NP // 2)
        step(NP - 1, 1, False, 0)


HALVES = 2
RT = H * S // HALVES // P
HB = 2 * HALVES
PTN = 4
K_STEPS, R_STEP = (2, 6), 4


def turn_order(hf, has_k):
    out = []
    for k in range(LT):
        out.append(("P", k))
        if hf == 0 and has_k and k in K_STEPS:
            out.append(("K", K_STEPS.index(k)))
        if k == R_STEP:
            out.append(("R", 0))
    return out


def turn_counts(has_k):
    at, split = {}, 0
    for hf in range(HALVES):
        for what in turn_order(hf, has_k):
            at[(hf, *what)] = (len(at), split)
            split += what[0] != "R"
    return at


TURNS, SPLITS = len(turn_counts(True)), sum(w[1] != "R" for w in turn_counts(True))


def build_cross(nc, ctx, sem, t, keep):
    ident, F, eps_pow = keep["ident"], keep["F"], keep["eps_pow"]
    kv_d, x_d, x1_d, h2_d = t["ctx"], t["x"], t["x1"], t["h2T"]
    qe_d = t["qe"].rearrange("a b d p x -> b d a (p x)")

    def sb(name, shape, dt=F32):
        return ctx.enter_context(nc.sbuf_tensor(name, shape, dt))

    kv, kr = keep["kv_raw"], keep["kv_rope"]
    KV = [Pair(ctx, nc, f"kv{j}", [P, LT, DC]) for j in range(2)]
    KT = [Pair(ctx, nc, f"kT{j}", [P, L]) for j in range(2)]
    QE = [ctx.enter_context(nc.sbuf_tensor(f"qe{j}", [P, 2, H * S], F32R)) for j in range(2)]
    PR = [sb(f"probs{j}", [P, RT, L]) for j in range(2)]
    PT = [Pair(ctx, nc, f"probsT{j}", [P, BANK]) for j in range(PTN)]
    CT = Pair(ctx, nc, "ctxT", [P, H, P])
    CX = sb("ctx_f32", [P, BANK])
    RB = sb("recip_rows", [P, BANK])
    XT, X1, HN = sb("x_tile", [P, D]), sb("x1_tile", [P, D]), sb("h2_tile", [P, D])
    H2 = sb("h2T_tile", [P, 2, D])
    nmax = [sb(f"nmax{j}", [P, RT]) for j in range(2)]
    rsum = [sb(f"rsum{j}", [P, RT]) for j in range(2)]
    rinv = sb("rinv", [P, RT])
    st, mv, var, rstd = sb("st2", [P, 6]), sb("mv2", [P, 2]), sb("var2", [P, 1]), sb("rstd2", [P, 1])

    psS = [ctx.enter_context(nc.psum_tensor(f"psS{j}", [P, L], F32)) for j in range(2)]
    psT = [ctx.enter_context(nc.psum_tensor(f"psTr{j}", [P, BANK], F32)) for j in range(2)]
    psV = ctx.enter_context(nc.psum_tensor("psV", [P, BANK], F32))
    psX = ctx.enter_context(nc.psum_tensor("psX", [P, BANK], F32))

    kv_in, xt_in, rope_done = keep["kv_in"], sem("xt_in"), keep["rope_done"]
    qe_in = [sem(f"qe_in{j}") for j in range(2)]
    kv_hi, kv_lo = sem("kv_hi"), sem("kv_lo")
    turned, turned_hi, turned_free = sem("turned"), sem("turned_hi"), sem("turned_free")
    recip_made, rows_made = sem("recip_made"), sem("rows_made")
    s_mm, max_made, exp_done = sem("s_mm"), sem("max_made"), sem("exp_done")
    pv_done = sem("pv_done")
    cx_done, ct_hi, ct_lo = sem("cx_done"), sem("ct_hi"), sem("ct_lo")
    proj_done, x1_made = sem("proj_done"), sem("x1_made")
    ln2, ln2_seen, rstd2, h2_made = sem("ln2"), sem("ln2_seen"), sem("rstd2"), sem("h2_made")
    h2_turned, h2_hi, h2_lo = sem("h2_turned"), sem("h2_hi"), sem("h2_lo")
    x1_out, h2_out = sem("x1_out"), sem("h2_out")

    AT = {True: turn_counts(True), False: turn_counts(False)}

    def place(b, hf, what, k, has_k):
        g, m = AT[has_k][(hf, what, k)]
        return 2 + TURNS * b + g + 1, 2 + SPLITS * b + m + 1, 2 + SPLITS * b + m + 1 + 2

    def half_steps(i, c, first, last):
        n, b = HB * i + c, 2 * i + c // 2
        has_k = not (last and c >= 2)
        more = not (last and c == 3)
        return n, b, c // 2, c % 2, has_k, more

    block = ctx.enter_context(nc.Block())

    @block.sync
    def _(sp):
        def load(b, j, i, first):
            if not (first and j == 0):
                sp.wait_ge(rope_done, b + 1)
                sp.dma_start(kv, kv_d[b]).then_inc(kv_in, 16)
            if not first:
                sp.wait_ge(s_mm, 8 * b - 8)
            sp.dma_start(QE[j][:].bitcast(F32), qe_d[b]).then_inc(qe_in[j], 16)
            if j == 1:
                sp.wait_ge(x1_made, i + 1)
                sp.dma_start(XT[:], x_d[i]).then_inc(xt_in, 16)

        for j in range(2):
            load(j, j, 0, True)
        with sp.Fori(1, B // 2) as i:
            for j in range(2):
                load(2 * i + j, j, i, False)
        sp.wait_ge(rope_done, B + 1)
        sp.dma_start(keep["early"][0], t["w_qkv"][0]).then_inc(keep["wqkv_in"][0], 16)
        sp.wait_ge(turned, place(B - 2, 0, "K", 1, True)[0])
        sp.wait_ge(kv_lo, B)
        sp.dma_start(keep["early"][1], t["w_qkv"][1]).then_inc(keep["wqkv_in"][1], 16)

    @block.gpsimd
    def _(pool):
        pool.sem_inc(ct_lo, 1)

        def kv_low(b, j):
            pool.wait_ge(kv_hi, b + 1)
            pool.tensor_tensor(KV[j].lo[:].rearrange("p l d -> p (l d)"), kr,
                               f32(KV[j].hi[:].rearrange("p l d -> p (l d)")), ALU.subtract).then_inc(kv_lo, 1)

        def ctx_low(n, c):
            cols = (slice((c % 2) * H // 2, (c % 2 + 1) * H // 2), slice((c // 2) * S, (c // 2 + 1) * S))
            pool.wait_ge(ct_hi, n + 1)
            pool.tensor_tensor(CT.lo[:, cols[0], cols[1]], CX[:].rearrange("p (h s) -> p h s", s=S),
                               f32(CT.hi[:, cols[0], cols[1]]), ALU.subtract).then_inc(ct_lo, 1)

        def root(tt):
            pool.wait_ge(ln2, 3 * tt + 3)
            pool.tensor_tensor(rstd[:], var[:], eps_pow[:], ALU.pow).then_inc(rstd2, 1)

        kv_low(0, 0)
        pool.wait_ge(turned, 2)
        pool.wait_ge(kv_lo, 1)
        rope_kv(pool, keep, 1)

        def iteration(i, first, last):
            for c in range(HB):
                n, b, j, hf, has_k, more = half_steps(i, c, first, last)
                if not (first and c == 0):
                    ctx_low(n - 1, (c - 1) % HB)
                if c == 1 and not first:
                    root(i - 1)
                if hf == 0 and has_k:
                    kv_low(b + 1, 1 - j)
                if hf == 1 and not last:
                    pool.wait_ge(turned, place(b, 0, "K", 1, True)[0])
                    pool.wait_ge(kv_lo, b + 2)
                    rope_kv(pool, keep, b + 2)

        iteration(0, True, False)
        with pool.Fori(1, NT - 1) as i:
            iteration(i, False, False)
        iteration(NT - 1, False, True)
        ctx_low(HB * NT - 1, HB - 1)
        root(NT - 1)

    @block.scalar
    def _(act):
        act.sem_inc(exp_done, 2)
        act.sem_inc(x1_out, 16)
        act.sem_inc(h2_out, 16)

        def kv_high(b, j):
            act.wait_ge(rope_done, b + 2)
            act.copy(KV[j].hi[:].rearrange("p l d -> p (l d)"), kr[:]).then_inc(kv_hi, 1)

        def exps(n, np_, rt):
            act.wait_ge(max_made, RT * n + rt + 1)
            act.activation(PR[np_][:, rt, :], psS[rt % 2][:], ACT.Exp, bias=nmax[np_][:, rt:rt + 1],
                           accum_out=rsum[np_][:, rt:rt + 1]).then_inc(exp_done, 1)

        def ctx_high(n, c, i):
            act.wait_ge(cx_done, n + 2)
            if c == 0:
                act.wait_ge(proj_done, i + 1)
            act.copy(CT.hi[:, (c % 2) * H // 2:(c % 2 + 1) * H // 2, (c // 2) * S:(c // 2 + 1) * S],
                     CX[:].rearrange("p (h s) -> p h s", s=S)).then_inc(ct_hi, 1)

        def store_x1(tt):
            act.wait_ge(x1_made, tt + 2)
            act.dma_start(x1_d[tt], X1[:]).then_inc(x1_out, 16)

        def h2_high(tt):
            act.wait_ge(h2_turned, tt + 1)
            act.wait_ge(h2_out, 16 * tt + 16)
            act.copy(H2[:, 0, :].bitcast(F32R), psX[:]).then_inc(h2_hi, 1)

        def store_h2(tt):
            act.wait_ge(h2_lo, tt + 2)
            act.dma_start(h2_d[tt], H2[:]).then_inc(h2_out, 16)

        for k in range(2):
            act.wait_ge(turned, k + 1)
            act.copy(KT[0].hi[:, k * BANK:(k + 1) * BANK], psT[k][:]).then_inc(turned_hi, 1)
        kv_high(0, 0)
        for rt in range(RT):
            exps(0, 0, rt)

        def iteration(i, first, last):
            for c in range(HB):
                n, b, j, hf, has_k, more = half_steps(i, c, first, last)
                for k in range(LT):
                    g = place(b, hf, "P", k, has_k)
                    slot = AT[has_k][(hf, "P", k)][0] % 2
                    act.wait_ge(turned, g[0])
                    act.wait_ge(pv_done, LT * n + k + 1)
                    act.copy(PT[k % PTN].hi[:], psT[slot][:]).then_inc(turned_hi, 1)
                    if hf == 0 and has_k and k in K_STEPS:
                        q = K_STEPS.index(k)
                        slot = AT[True][(0, "K", q)][0] % 2
                        act.wait_ge(turned, place(b, 0, "K", q, True)[0])
                        act.copy(KT[1 - j].hi[:, q * BANK:(q + 1) * BANK], psT[slot][:]).then_inc(turned_hi, 1)
                    if k == 1 and not (first and c == 0):
                        ctx_high(n - 1, (c - 1) % HB, i)
                    if k == 3 and hf == 0 and has_k:
                        kv_high(b + 1, 1 - j)
                    if k == R_STEP:
                        g = place(b, hf, "R", 0, has_k)
                        slot = AT[has_k][(hf, "R", 0)][0] % 2
                        act.wait_ge(turned, g[0])
                        act.copy(RB[:], psT[slot][:]).then_inc(rows_made, 1)
                    if k % 2 == 1 and more:
                        exps(n + 1, (c + 1) % 2, k // 2)
                    if not first:
                        if (c, k) == (1, 5):
                            store_x1(i - 1)
                        if (c, k) == (2, 6):
                            h2_high(i - 1)
                        if (c, k) == (3, 1):
                            store_h2(i - 1)

        iteration(0, True, False)
        with act.Fori(1, NT - 1) as i:
            iteration(i, False, False)
        iteration(NT - 1, False, True)
        ctx_high(HB * NT - 1, HB - 1, NT - 1)
        store_x1(NT - 1)
        h2_high(NT - 1)
        store_h2(NT - 1)
        act.wait_ge(x1_out, 16 * NT + 16)
        act.wait_ge(h2_out, 16 * NT + 16)

    @block.vector
    def _(dve):
        dve.sem_inc(turned_free, 2)
        dve.sem_inc(cx_done, 1)
        dve.sem_inc(x1_made, 1)
        dve.sem_inc(h2_lo, 1)

        def maxes(n, np_, rt):
            dve.wait_ge(s_mm, RT * n + rt + 1)
            dve.tensor_reduce(nmax[np_][:, rt:rt + 1], psS[rt % 2][:], AX.X, ALU.max,
                              negate=True).then_inc(max_made, 1)

        def lo_part(hi_count, out, slot, hi):
            dve.wait_ge(turned_hi, hi_count)
            dve.tensor_tensor(out, psT[slot][:], f32(hi), ALU.subtract).then_inc(turned_free, 1)

        def residual(tt):
            dve.wait_ge(proj_done, tt + 2)
            dve.wait_ge(xt_in, 16 * tt + 16)
            dve.wait_ge(x1_out, 16 * tt + 16)
            dve.tensor_tensor(X1[:], psX[:], XT[:], ALU.add).then_inc(x1_made, 1)

        def stats(tt):
            dve.wait_ge(x1_made, tt + 2)
            dve.bn_stats(st[:], X1[:]).then_inc(ln2, 1)

        def aggregate(tt):
            dve.wait_ge(ln2, 3 * tt + 1)
            dve.sem_inc(ln2_seen, 1)
            dve.bn_aggr(mv[:], st[:]).then_inc(ln2, 1)

        def variance(tt):
            dve.wait_ge(ln2, 3 * tt + 2)
            dve.tensor_scalar(var[:], mv[:, 1:2], EPS, None, ALU.add).then_inc(ln2, 1)

        def norm(tt):
            dve.wait_ge(rstd2, tt + 1)
            dve.tensor_scalar(HN[:], X1[:], mv[:, 0:1], rstd[:], ALU.subtract, ALU.mult).then_inc(h2_made, 1)

        def h2_low(tt):
            dve.wait_ge(h2_hi, tt + 1)
            dve.tensor_tensor(H2[:, 1, :].bitcast(F32R), psX[:], H2[:, 0, :], ALU.subtract).then_inc(h2_lo, 1)

        LN_STEPS = {1: residual, 3: stats, 4: aggregate, 5: variance}

        for k in range(2):
            cols = slice(k * BANK, (k + 1) * BANK)
            lo_part(k + 1, KT[0].lo[:, cols], k, KT[0].hi[:, cols])
        for rt in range(RT):
            maxes(0, 0, rt)

        def iteration(i, first, last):
            for c in range(HB):
                n, b, j, hf, has_k, more = half_steps(i, c, first, last)
                for k in range(LT):
                    g = place(b, hf, "P", k, has_k)
                    lo_part(g[1], PT[k % PTN].lo[:], AT[has_k][(hf, "P", k)][0] % 2, PT[k % PTN].hi[:])
                    if k == 2:
                        dve.wait_ge(exp_done, RT * n + RT + 2)
                        dve.reciprocal(rinv[:], rsum[c % 2][:]).then_inc(recip_made, 1)
                    if k % 2 == 0 and more:
                        maxes(n + 1, (c + 1) % 2, k // 2)
                    if hf == 0 and has_k and k in K_STEPS:
                        q = K_STEPS.index(k)
                        cols = slice(q * BANK, (q + 1) * BANK)
                        lo_part(place(b, 0, "K", q, True)[1], KT[1 - j].lo[:, cols],
                                AT[True][(0, "K", q)][0] % 2, KT[1 - j].hi[:, cols])
                    if not first:
                        if c == 1 and k in LN_STEPS:
                            LN_STEPS[k](i - 1)
                        if (c, k) == (2, 1):
                            norm(i - 1)
                        if (c, k) == (2, 7):
                            h2_low(i - 1)
                dve.wait_ge(rows_made, n + 1)
                dve.wait_ge(pv_done, LT * n + LT + PTN)
                dve.wait_ge(ct_lo, n + 1)
                dve.tensor_tensor(CX[:], psV[:], RB[:], ALU.mult).then_inc(cx_done, 1)

        iteration(0, True, False)
        with dve.Fori(1, NT - 1) as i:
            iteration(i, False, False)
        iteration(NT - 1, False, True)
        for part in LN_STEPS.values():
            part(NT - 1)
        norm(NT - 1)
        h2_low(NT - 1)

    @block.tensor
    def _(pe):
        pe.sem_inc(pv_done, PTN)
        pe.sem_inc(proj_done, 1)

        def scores(n, j, hf, rt):
            pe.wait_ge(exp_done, RT * n + rt + 1)
            rows = slice(hf * BANK + rt * P, hf * BANK + (rt + 1) * P)
            for half in range(2):
                cols = slice(half * BANK, (half + 1) * BANK)
                last = mm3(pe, psS[rt % 2][:, cols], (QE[j][:, 0, rows], QE[j][:, 1, rows]),
                           KT[j].at(ALL, cols), True, True)
            last.then_inc(s_mm, 1)

        def turn(slot, src):
            for q in range(BANK // P):
                last = pe.transpose(psT[slot][:, q * P:(q + 1) * P], src(q), ident[:])
            last.then_inc(turned, 1)

        def slot_free(b, hf, what, k, has_k):
            at = AT[has_k]
            g = at[(hf, what, k)][0]
            if g < 2:
                pe.wait_ge(turned_free, 2 + SPLITS * b + g - 2 + 1 + 2)
            else:
                before = next(w for w in at if at[w][0] == g - 2)
                if before[1] == "R":
                    pe.wait_ge(rows_made, HALVES * b + before[0] + 1)
                else:
                    pe.wait_ge(turned_free, place(b, *before, has_k)[2])
            return g % 2

        def project(tt, heads):
            for h in heads:
                if h == 0:
                    pe.wait_ge(h2_lo, tt + 1)
                    pe.wait_ge(ct_lo, HB * tt + HB)
                if h == H // 2:
                    pe.wait_ge(ct_lo, HB * tt + HB + 1)
                last = mm3(pe, psX[:], CT.at(ALL, h, ALL), F.at(ALL, h, ALL), h == 0, h == H - 1)
            if h == H - 1:
                last.then_inc(proj_done, 1)

        def turn_h2(tt):
            pe.wait_ge(h2_made, tt + 1)
            for k in range(KC):
                last = pe.transpose(psX[:, k * P:(k + 1) * P], HN[:, k * P:(k + 1) * P], ident[:])
            last.then_inc(h2_turned, 1)

        pe.wait_ge(rope_done, 2)
        for k in range(2):
            turn(k, lambda q: kr[:, (4 * k + q) * P:(4 * k + q + 1) * P])
        pe.wait_ge(turned_free, 4)
        pe.wait_ge(qe_in[0], 16)
        for rt in range(RT):
            scores(0, 0, 0, rt)

        def iteration(i, first, last):
            for c in range(HB):
                n, b, j, hf, has_k, more = half_steps(i, c, first, last)
                for k in range(LT):
                    if k == 0:
                        pe.wait_ge(exp_done, RT * n + RT + 2)
                    turn(slot_free(b, hf, "P", k, has_k), lambda q: PR[c % 2][:, q, k * P:(k + 1) * P])
                    if k % 2 == 0 and more:
                        if hf == 1 and k == 0:
                            pe.wait_ge(turned_free, place(b, 0, "K", 1, True)[2])
                            pe.wait_ge(qe_in[1 - j], 16 * (i + 1 + j))
                        scores(n + 1, j if hf == 0 else 1 - j, 1 - hf, k // 2)
                    if hf == 0 and has_k and k in K_STEPS:
                        at = 4 * K_STEPS.index(k)
                        if at == 0:
                            pe.wait_ge(rope_done, b + 3)
                        turn(slot_free(b, 0, "K", at // 4, True), lambda q: kr[:, (at + q) * P:(at + q + 1) * P])
                    if k == R_STEP:
                        pe.wait_ge(recip_made, n + 1)
                        turn(slot_free(b, hf, "R", 0, has_k), lambda q: rinv[:, q:q + 1].to_broadcast([P, P]))
                    for kk in ([k - 2] if k in range(2, LT - 1) else [LT - 3, LT - 2, LT - 1] if k == LT - 1 else []):
                        pe.wait_ge(turned_free, place(b, hf, "P", kk, has_k)[2])
                        if kk == 0:
                            pe.wait_ge(cx_done, n + 1)
                            pe.wait_ge(kv_lo, b + 1)
                        mm3(pe, psV[:], KV[j].at(ALL, kk, ALL), PT[kk % PTN].at(ALL, ALL),
                            kk == 0, kk == LT - 1).then_inc(pv_done, 1)
                    if not first:
                        if c == 0:
                            project(i - 1, range(2 * k, 2 * k + 2))
                        if (c, k) == (2, 5):
                            turn_h2(i - 1)
                    if last and c == 3 and k >= 2:
                        project(i, range(max(0, k - 2) + min(k - 2, 2), k - 1 + min(k - 1, 2)))

        iteration(0, True, False)
        with pe.Fori(1, NT - 1) as i:
            iteration(i, False, False)
        iteration(NT - 1, False, True)
        project(NT - 1, range(H // 2, H))
        turn_h2(NT - 1)


NGRP = NT * HKV
WCH = 5
GI = 2 * HKV


def wait(eng, sem, value):
    if not isinstance(value, int) or value > 0:
        eng.wait_ge(sem, value)


def build_self(nc, ctx, sem, t, keep):
    ident, wo_in = keep["ident"], keep["wo_in"]

    def sb(name, shape, dt=F32):
        return ctx.enter_context(nc.sbuf_tensor(name, shape, dt))

    W = Pair(ctx, nc, "wqkv", [P, WCH, KC, BANK])
    raw = keep["early"] + keep["ahead"][:WCH - 2]
    tab = sb("rope_s_tab", [P, 2, 3, DH // 2])
    mask_f, mask = sb("mask_f", [P, BANK]), sb("mask_r", [P, BANK], F32R)
    ident_r = sb("ident_r", [P, P], F32R)
    HT = [sb(f"h2T{j}", [P, 2, KC, P], F32R) for j in range(2)]
    QR = sb("q_terms", [P, 2, BANK])
    KR = sb("k_terms", [P, 2, HKV * DH])
    QN, KN = sb("q_rope", [P, BANK]), sb("k_rope", [P, HKV * DH])
    QB = [sb(f"qT{j}", [P, REP, 2, S]) for j in range(2)]
    KB = [sb(f"kTs{j}", [P, HKV, S]) for j in range(2)]
    VB = [Pair(ctx, nc, f"v_pairs{j}", [P, 2, HKV, 2, DH]) for j in range(2)]
    PR = [sb(f"sprobs{j}", [P, REP, S]) for j in range(2)]
    PT = [Pair(ctx, nc, f"sprobsT{j}", [P, REP // 2, P]) for j in range(2)]
    AO = [sb(f"attn_out{j}", [P, BANK]) for j in range(2)]
    nmax = [sb(f"snmax{j}", [P, REP]) for j in range(2)]
    rsum = [sb(f"srsum{j}", [P, REP]) for j in range(2)]
    rinv = [sb(f"srinv{j}", [P, REP]) for j in range(2)]

    psS = [ctx.enter_context(nc.psum_tensor(f"psSs{j}", [P, REP, S], F32)) for j in range(2)]
    psP = ctx.enter_context(nc.psum_tensor("psP", [P, REP // 2, P], F32))
    psQ = ctx.enter_context(nc.psum_tensor("psQs", [P, BANK], F32))
    psK = ctx.enter_context(nc.psum_tensor("psK", [P, BANK], F32))
    psT, psTk = (ctx.enter_context(nc.psum_tensor(n, [P, BANK], F32)) for n in ("psTq", "psTk"))
    psO = ctx.enter_context(nc.psum_tensor("psO", [P, BANK], F32))

    w_in = keep["wqkv_in"]
    tab_in = sem("tabs_in")
    ht_in = [sem(f"ht_in{j}") for j in range(2)]
    w_hi, w_ready = sem("wqkv_hi"), sem("wqkv_ready")
    zeroed, consts = sem("zeroed"), sem("consts")
    kv_mm, q_mm = sem("skv_mm"), sem("sq_mm")
    k_terms, q_terms, k_roped, q_roped = sem("k_terms"), sem("q_terms"), sem("k_roped"), sem("q_roped")
    t_mm, t_out = sem("st_mm"), sem("st_out")
    v_hi, v_lo = sem("sv_hi"), sem("sv_lo")
    s_mm, max_made, exp_done = sem("ss_mm"), sem("smax_made"), sem("sexp_done")
    recip_made, normed = sem("srecip_made"), sem("normed")
    p_mm, p_hi, p_lo = sem("sp_mm"), sem("sp_hi"), sem("sp_lo")
    pv_mm, ao_made = sem("spv_mm"), sem("ao_made")
    ao_out = [sem(f"ao_out{j}") for j in range(2)]

    def order_k(tt):
        return (HKV + 1) * tt

    def order_q(tt, g):
        return (HKV + 1) * tt + g + 1

    def halves(ap):
        return ap.rearrange("p (h two x) -> p h two x", two=2, x=DH // 2)

    def plan(i, v, last):
        def ahead(k):
            return not last or v + k < GI
        return GI * i + v, 2 * i + v // HKV, v % HKV, ahead

    def turns(eng, step):
        for v in range(GI):
            step(0, v, False)
        with eng.Fori(1, NT // 2 - 1) as i:
            for v in range(GI):
                step(i, v, False)
        for v in range(GI):
            step(NT // 2 - 1, v, True)

    block = ctx.enter_context(nc.Block())

    @block.sync
    def _(sp):
        sp.dma_start(HT[0][:].bitcast(F32).rearrange("p a k x -> p a (k x)"), t["h2T"][0]).then_inc(ht_in[0], 16)
        sp.dma_start(tab[:], t["rope_s"]).then_inc(tab_in, 16)
        sp.dma_start(mask_f[:], t["mask"]).then_inc(tab_in, 16)
        for c in range(2, WCH):
            sp.dma_start(raw[c], t["w_qkv"][c]).then_inc(w_in[c], 16)
        sp.dma_start(HT[1][:].bitcast(F32).rearrange("p a k x -> p a (k x)"), t["h2T"][1]).then_inc(ht_in[1], 16)
        for c in range(W_AHEAD):
            if c < WCH - 2:
                sp.wait_ge(w_ready, c + 3)
            sp.dma_start(keep["ahead"][c], t["w_o"][:, c * KC:(c + 1) * KC, :]).then_inc(wo_in[c], 16)

        def step(i, v, last):
            u, tt, g, ahead = plan(i, v, last)
            if last and v == 2:
                for j in range(2):
                    sp.wait_ge(ao_out[j], 16 * HKV)
                for j in range(2):
                    sp.dma_start(keep["early"][j].rearrange("p k c -> p (k c)"),
                                 t["ao"][j].rearrange("p h x -> p (h x)")).then_inc(keep["a_in"][j], 16)
            if g == 1 and ahead(GI):
                sp.wait_ge(q_mm, u + 3)
                sp.dma_start(HT[v // HKV][:].bitcast(F32).rearrange("p a k x -> p a (k x)"),
                             t["h2T"][tt + 2]).then_inc(ht_in[v // HKV], 16)
            if not (isinstance(u, int) and u == 0):
                store(u - 1, tt if g else tt - 1, (g - 1) % HKV, (v - 1) % 2)

        def store(u, tt, g, j):
            sp.wait_ge(ao_made, u + 1)
            sp.dma_start(t["ao"][tt, :, g * KC:(g + 1) * KC, :],
                         AO[j][:].rearrange("p (a x) -> p a x", x=P)).then_inc(ao_out[j], 16)

        turns(sp, step)
        store(NGRP - 1, NT - 1, HKV - 1, 1)
        for j in range(2):
            sp.wait_ge(ao_out[j], 16 * NGRP // 2)

    @block.gpsimd
    def _(pool):
        for j in range(2):
            pool.memset(QB[j][:], 0.0).then_inc(zeroed, 1)
            pool.memset(f32(VB[j].hi[:]), 0.0).then_inc(zeroed, 1)
            pool.memset(f32(VB[j].lo[:]), 0.0).then_inc(zeroed, 1)

        def rope_k(tt):
            pool.wait_ge(k_terms, 3 * tt + 3)
            wait(pool, t_mm, order_k(tt - 1) + 1)
            pool.tensor_tensor(KN[:], KR[:, 0], KR[:, 1], ALU.add).then_inc(k_roped, 1)

        def rope_q(u, tt, g):
            pool.wait_ge(q_terms, 3 * u + 3)
            pool.wait_ge(t_mm, order_q(tt, g) - (1 if g else 2) + 1)
            pool.tensor_tensor(QN[:], QR[:, 0], QR[:, 1], ALU.add).then_inc(q_roped, 1)

        def norm(u, j):
            pool.wait_ge(recip_made, u + 1)
            pool.tensor_tensor(PR[j][:], PR[j][:], rinv[j][:].unsqueeze(2).to_broadcast([P, REP, S]),
                               ALU.mult).then_inc(normed, 1)

        rope_k(0)
        pool.wait_ge(q_terms, 3)
        pool.tensor_tensor(QN[:], QR[:, 0], QR[:, 1], ALU.add).then_inc(q_roped, 1)
        rope_q(1, 0, 1)
        norm(0, 0)
        rope_q(2, 0, 2)

        def step(i, v, last):
            u, tt, g, ahead = plan(i, v, last)
            if ahead(3):
                if g == 1:
                    rope_k(tt + 1)
                rope_q(u + 3, tt + (g + 3) // HKV, (g + 3) % HKV)
            if ahead(1):
                norm(u + 1, (v + 1) % 2)

        turns(pool, step)

    @block.scalar
    def _(act):
        def high(c):
            act.wait_ge(w_in[c], 16)
            act.copy(W.hi[:, c], raw[c]).then_inc(w_hi, 1)

        def turned(order, dst, n):
            act.wait_ge(t_mm, order + 1)
            src = (psT if n == REP else psTk)[:, 0:n * DH].rearrange("p (h b s) -> p h b s", b=2, s=S)
            for a in range(2):
                for b in range(2):
                    rows = slice(b * DH, (b + 1) * DH)
                    to = dst[rows, a:n:2, b, :] if n == REP else dst[rows, a:n:2, :]
                    act.copy(to, src[a * DH:(a + 1) * DH, :, b, :]).then_inc(t_out, 1)

        def exps(u, j):
            act.wait_ge(max_made, u + 1)
            for h in range(REP):
                act.activation(PR[j][:, h, :], psS[j][:, h, :], ACT.Exp, bias=nmax[j][:, h:h + 1],
                               accum_out=rsum[j][:, h:h + 1]).then_inc(exp_done, 1)

        def v_high(tt, dst):
            act.wait_ge(k_terms, 3 * tt + 3)
            wait(act, pv_mm, HKV * (tt - 1))
            for b in range(2):
                v = psK[b * S:(b + 1) * S, HKV * DH:].rearrange("p (g x) -> p g x", x=DH)
                for a in range(2):
                    act.copy(dst.hi[a * S:(a + 1) * S, b, :, a, :], v).then_inc(v_hi, 1)

        def attn_out(u, i, v):
            act.wait_ge(pv_mm, u + 1)
            wait(act, ao_out[v % 2], 16 * (GI // 2 * i + v // 2))
            act.copy(AO[v % 2][:], psO[:]).then_inc(ao_made, 1)

        high(0)
        high(1)
        act.wait_ge(tab_in, 32)
        act.copy(mask[:], mask_f[:]).then_inc(consts, 1)
        act.copy(ident_r[:], ident[:]).then_inc(consts, 1)
        high(2)
        act.wait_ge(zeroed, 6)
        turned(order_k(0), KB[0], HKV)
        turned(order_q(0, 0), QB[0], REP)
        high(3)
        exps(0, 0)
        turned(order_q(0, 1), QB[1], REP)
        v_high(0, VB[0])
        high(4)

        def step(i, v, last):
            u, tt, g, ahead = plan(i, v, last)
            if g == 1 and ahead(3):
                v_high(tt + 1, VB[1 - v // HKV])
            if ahead(2):
                if g == 2:
                    turned(order_k(tt + 1), KB[1 - v // HKV], HKV)
                turned(order_q(tt + (g + 2) // HKV, (g + 2) % HKV), QB[v % 2], REP)
            act.wait_ge(p_mm, u + 1)
            wait(act, pv_mm, u - 1)
            act.copy(PT[v % 2].hi[:], psP[:]).then_inc(p_hi, 1)
            if ahead(1):
                exps(u + 1, (v + 1) % 2)
            if not (isinstance(u, int) and u == 0):
                attn_out(u - 1, i if v else i - 1, (v - 1) % GI)

        turns(act, step)
        attn_out(NGRP - 1, NT // 2 - 1, GI - 1)

    @block.vector
    def _(dve):
        def terms(src, dst, rows, scaled, made):
            x, cs, sn = halves(src), halves(dst[:, 0]), halves(dst[:, 1])
            n = rows
            c = tab[:, scaled, 0, :].unsqueeze(1).to_broadcast([P, 2 * n, DH // 2])
            dve.tensor_tensor(cs.rearrange("p h two x -> p (h two) x"), x.rearrange("p h two x -> p (h two) x"),
                              c, ALU.mult).then_inc(made, 1)
            for a in range(2):
                s = tab[:, scaled, 1 + a, :].unsqueeze(1).to_broadcast([P, n, DH // 2])
                dve.tensor_tensor(sn[:, :, a, :], x[:, :, 1 - a, :], s, ALU.mult).then_inc(made, 1)

        def terms_k(tt):
            dve.wait_ge(kv_mm, tt + 1)
            wait(dve, k_roped, tt)
            terms(psK[:, 0:HKV * DH], KR, HKV, 1, k_terms)

        def terms_q(u):
            dve.wait_ge(q_mm, u + 1)
            wait(dve, q_roped, u)
            terms(psQ[:], QR, REP, 0, q_terms)

        def low(c):
            dve.wait_ge(w_hi, c + 1)
            dve.tensor_tensor(W.lo[:, c], raw[c], f32(W.hi[:, c]), ALU.subtract).then_inc(w_ready, 1)

        def maxes(u, j):
            dve.wait_ge(s_mm, u + 1)
            dve.tensor_reduce(nmax[j][:], psS[j][:], AX.X, ALU.max, negate=True).then_inc(max_made, 1)

        def recips(u, j):
            dve.wait_ge(exp_done, REP * (u + 1))
            dve.reciprocal(rinv[j][:], rsum[j][:]).then_inc(recip_made, 1)

        def v_low(tt, dst):
            dve.wait_ge(v_hi, 4 * tt + 4)
            for b in range(2):
                v = psK[b * S:(b + 1) * S, HKV * DH:].rearrange("p (g x) -> p g x", x=DH)
                for a in range(2):
                    rows = slice(a * S, (a + 1) * S)
                    dve.tensor_tensor(dst.lo[rows, b, :, a, :], v, f32(dst.hi[rows, b, :, a, :]),
                                      ALU.subtract).then_inc(v_lo, 1)

        low(0)
        low(1)
        dve.wait_ge(tab_in, 32)
        terms_k(0)
        terms_q(0)
        low(2)
        terms_q(1)
        low(3)
        maxes(0, 0)
        v_low(0, VB[0])
        terms_q(2)
        low(4)
        recips(0, 0)

        def step(i, v, last):
            u, tt, g, ahead = plan(i, v, last)
            if ahead(3):
                if g == 1:
                    terms_k(tt + 1)
                terms_q(u + 3)
            if ahead(1):
                maxes(u + 1, (v + 1) % 2)
            dve.wait_ge(p_hi, u + 1)
            dve.tensor_tensor(PT[v % 2].lo[:], psP[:], f32(PT[v % 2].hi[:]), ALU.subtract).then_inc(p_lo, 1)
            if ahead(1):
                recips(u + 1, (v + 1) % 2)
            if g == 1 and ahead(3):
                v_low(tt + 1, VB[1 - v // HKV])

        turns(dve, step)

    @block.tensor
    def _(pe):
        def product(tt, j, n, c, out, made):
            pe.wait_ge(w_ready, c + 1)
            pe.wait_ge(ht_in[j], 16 * n)
            for k in range(KC):
                last = mm3(pe, out, (HT[j][:, 0, k, :], HT[j][:, 1, k, :]), W.at(ALL, c, k, ALL),
                           k == 0, k == KC - 1)
            last.then_inc(made, 1)

        def product_kv(tt, j, n):
            wait(pe, v_lo, 4 * tt)
            wait(pe, k_terms, 3 * tt)
            product(tt, j, n, 0, psK[:], kv_mm)

        def product_q(u, tt, j, n, g):
            wait(pe, q_terms, 3 * u)
            product(tt, j, n, 1 + g, psQ[:], q_mm)

        def turn(dst, src, n, made, count, before):
            pe.wait_ge(made, count)
            wait(pe, t_out, before)
            for q in range(n // 2):
                last = pe.transpose(dst[:, q * P:(q + 1) * P], src[:, q * P:(q + 1) * P], ident[:])
            last.then_inc(t_mm, 1)

        def turn_k(tt):
            turn(psTk, KN, HKV, k_roped, tt + 1, 4 * order_k(tt - 1) + 4)

        def turn_q(u, tt, g):
            turn(psT, QN, REP, q_roped, u + 1, 4 * (order_q(tt, g) - (1 if g else 2)) + 4)

        def scores_mask(u, tt, g, j):
            pe.wait_ge(t_out, 4 * order_q(tt, g) + 4)
            wait(pe, exp_done, REP * (u - 1))
            pe.matmul(psS[j][:], ident_r[:], mask[:], start=True, stop=False, skip_group_check=True)

        def scores(g, j, kt, heads):
            for h in heads:
                last = pe.matmul(psS[j][:, h, :], QB[j][:, h].rearrange("p b s -> p (b s)"), KB[kt][:, g, :],
                                 start=False, stop=h == REP - 1, skip_group_check=True)
            if heads[-1] == REP - 1:
                last.then_inc(s_mm, 1)

        def turn_probs(u, j):
            pe.wait_ge(normed, u + 1)
            wait(pe, p_lo, u)
            for h in range(REP // 2):
                last = pe.transpose(psP[:, h, :], PR[j][:, 2 * h:2 * h + 2, :].rearrange("p a s -> p (a s)"), ident[:])
            last.then_inc(p_mm, 1)

        def values(u, tt, g, j, v_of):
            pe.wait_ge(p_lo, u + 1)
            pe.wait_ge(v_lo, 4 * tt + 4)
            wait(pe, ao_made, u)
            for b in range(2):
                tokens = slice(b * S, (b + 1) * S)
                v = tuple(part[:, b, g].rearrange("p a d -> p (a d)") for part in (v_of.hi, v_of.lo))
                last = mm3(pe, psO[:].rearrange("p (h t) -> p h t", t=P)[:, :, tokens], v,
                           PT[j].at(ALL, ALL, tokens), True, True)
            last.then_inc(pv_mm, 1)

        product_kv(0, 0, 1)
        product_q(0, 0, 0, 1, 0)
        turn_k(0)
        turn_q(0, 0, 0)
        product_q(1, 0, 0, 1, 1)
        pe.wait_ge(consts, 2)
        scores_mask(0, 0, 0, 0)
        scores(0, 0, 0, range(REP))
        turn_q(1, 0, 1)
        product_q(2, 0, 0, 1, 2)

        def step(i, v, last):
            u, tt, g, ahead = plan(i, v, last)
            g1, kt1 = (g + 1) % HKV, (v + 1) // HKV % 2
            t3, g3 = tt + (g + 3) // HKV, (g + 3) % HKV
            j3, n3 = (v + 3) // HKV % 2, i + 1 + (v + 3) // GI
            if ahead(3):
                if g == 1:
                    product_kv(t3, j3, n3)
                wait(pe, q_terms, 3 * (u + 3))
                pe.wait_ge(w_ready, g3 + 2)
                pe.wait_ge(ht_in[j3], 16 * n3)
            for k in range(KC):
                if ahead(3):
                    last_q = mm3(pe, psQ[:], (HT[j3][:, 0, k, :], HT[j3][:, 1, k, :]), W.at(ALL, 1 + g3, k, ALL),
                                 k == 0, k == KC - 1)
                    if k == KC - 1:
                        last_q.then_inc(q_mm, 1)
                if ahead(1) and k == 0:
                    scores_mask(u + 1, tt + (g + 1) // HKV, g1, (v + 1) % 2)
                if ahead(1):
                    scores(g1, (v + 1) % 2, kt1, range(2 * k, 2 * k + 2))
            if ahead(2):
                if g == 2:
                    turn_k(tt + 1)
                turn_q(u + 2, tt + (g + 2) // HKV, (g + 2) % HKV)
            turn_probs(u, v % 2)
            if not (isinstance(u, int) and u == 0):
                values(u - 1, tt if g else tt - 1, (g - 1) % HKV, (v - 1) % 2, VB[(v - 1) // HKV % 2])

        turns(pe, step)
        values(NGRP - 1, NT - 1, HKV - 1, 1, VB[1])


def build_project(nc, ctx, sem, t, keep):
    ident, eps_pow, acc, h3T = keep["ident"], keep["eps_pow"], keep["acc"], keep["h3T"]
    w_in, wexp_in, gate_in, gate_f = keep["wo_in"], keep["wexp_in"], keep["gate_in"], keep["gate_f"]
    nh = HQ // 2
    wc = KC

    def sb(name, shape, dt=F32):
        return ctx.enter_context(nc.sbuf_tensor(name, shape, dt))

    W = Pair(ctx, nc, "wo", [P, nh, D])
    raw = keep["ahead"]
    A = [e.rearrange("p k (a x) -> p (k a) x", x=P) for e in keep["early"]]
    AS = [Pair(ctx, nc, f"ao_parts{j}", [P, nh, P]) for j in range(2)]
    X1 = [sb(f"x1_in{j}", [P, D]) for j in range(2)]
    HN = [sb(f"h3_tile{j}", [P, D]) for j in range(2)]
    st = [sb(f"st3_{j}", [P, 6]) for j in range(2)]
    mv = [sb(f"mv3_{j}", [P, 2]) for j in range(2)]
    var = [sb(f"var3_{j}", [P, 1]) for j in range(2)]
    rstd = [sb(f"rstd3_{j}", [P, 1]) for j in range(2)]
    psX = [ctx.enter_context(nc.psum_tensor(f"psX4_{j}", [P, BANK], F32)) for j in range(2)]
    psH = [ctx.enter_context(nc.psum_tensor(f"psH4_{j}", [P, BANK], F32)) for j in range(2)]

    a_in = keep["a_in"]
    x_in = [sem(f"x1_in{j}") for j in range(2)]
    w_hi, w_ready = sem("wo_hi"), sem("wo_ready")
    a_hi, a_lo, proj, x2_made = sem("a_hi"), sem("a_lo"), sem("proj"), sem("x2_made")
    ln3, ln3_seen, rstd3, h3_made = sem("ln3"), sem("ln3_seen"), sem("rstd3"), sem("h3_made")
    h3_turned, h3_hi, h3_lo = sem("h3_turned"), sem("h3_hi"), sem("h3_lo")

    def tiles(eng, step):
        for j in range(2):
            step(j, j, 0, True)
        with eng.Fori(1, NT // 2 - 1) as i:
            for j in range(2):
                step(2 * i + j, j, i, True)
        for j in range(2):
            step(NT - 2 + j, j, NT // 2 - 1, j == 0)

    block = ctx.enter_context(nc.Block())

    @block.sync
    def _(sp):
        def load(tt, j, first=False):
            if not first:
                sp.dma_start(A[j], t["ao"][tt]).then_inc(a_in[j], 16)
            sp.dma_start(X1[j][:], t["x1"][tt]).then_inc(x_in[j], 16)

        load(0, 0, True)
        load(1, 1, True)
        sp.dma_start(gate_f[:], t["gate_w"]).then_inc(gate_in, 16)
        sp.wait_ge(w_ready, nh // wc)
        for j in range(2):
            sp.dma_start(keep["w_ahead"][j], t["w_exp"][j]).then_inc(wexp_in[j], 16)
        with sp.Fori(1, NT // 2) as i:
            for j in range(2):
                sp.wait_ge(a_lo, 2 * i + j - 1)
                sp.wait_ge(x2_made, 2 * i + j - 1)
                load(2 * i + j, j)

    @block.gpsimd
    def _(pool):
        def split(tt, j):
            pool.wait_ge(a_hi, tt + 1)
            pool.tensor_tensor(AS[j].lo[:], A[j], f32(AS[j].hi[:]), ALU.subtract).then_inc(a_lo, 1)

        def step(tt, j, i, more):
            if more:
                split(tt + 1, 1 - j)
            pool.wait_ge(ln3, 3 * tt + 3)
            pool.tensor_tensor(rstd[j][:], var[j][:], eps_pow[:], ALU.pow).then_inc(rstd3, 1)

        pool.wait_ge(a_lo, 1)
        tiles(pool, step)

    @block.scalar
    def _(act):
        def split(tt, j, n):
            act.wait_ge(a_in[j], 16 * n)
            wait(act, proj, tt - 1)
            act.copy(AS[j].hi[:], A[j]).then_inc(a_hi, 1)

        def turned(tt, j):
            act.wait_ge(h3_turned, tt + 1)
            act.copy(h3T.hi[:, :, bass.ds(tt * P, P)], psH[j][:].rearrange("p (k x) -> p k x", k=KC)).then_inc(h3_hi, 1)

        def step(tt, j, i, more):
            if more:
                split(tt + 1, 1 - j, i + 1 + j)
            if not (isinstance(tt, int) and tt == 0):
                turned(tt - 1, 1 - j)

        for c in range(nh // wc):
            act.wait_ge(w_in[c], 16)
            act.copy(W.hi[:, c * wc:(c + 1) * wc, :], raw[c]).then_inc(w_hi, 1)
            if c == 0:
                split(0, 0, 1)
        tiles(act, step)
        turned(NT - 1, 1)

    @block.vector
    def _(dve):
        def turned(tt, j):
            dst = bass.ds(tt * P, P)
            dve.wait_ge(h3_hi, tt + 1)
            dve.tensor_tensor(h3T.lo[:, :, dst], psH[j][:].rearrange("p (k x) -> p k x", k=KC),
                              f32(h3T.hi[:, :, dst]), ALU.subtract).then_inc(h3_lo, 1)

        def step(tt, j, i, more):
            x2 = acc[:, bass.ds(tt, 1), :].rearrange("p o c -> p (o c)")
            dve.wait_ge(proj, tt + 1)
            dve.wait_ge(x_in[j], 16 * (i + 1))
            dve.tensor_tensor(x2, psX[j][:], X1[j][:], ALU.add).then_inc(x2_made, 1)
            dve.wait_ge(x2_made, tt + 1)
            dve.sem_inc(ln3_seen, 1)
            dve.bn_stats(st[j][:], x2).then_inc(ln3, 1)
            dve.wait_ge(ln3, 3 * tt + 1)
            dve.sem_inc(ln3_seen, 1)
            dve.bn_aggr(mv[j][:], st[j][:]).then_inc(ln3, 1)
            dve.wait_ge(ln3, 3 * tt + 2)
            dve.tensor_scalar(var[j][:], mv[j][:, 1:2], EPS, None, ALU.add).then_inc(ln3, 1)
            if not (isinstance(tt, int) and tt == 0):
                turned(tt - 1, 1 - j)
            dve.wait_ge(rstd3, tt + 1)
            dve.tensor_scalar(HN[j][:], x2, mv[j][:, 0:1], rstd[j][:], ALU.subtract, ALU.mult).then_inc(h3_made, 1)

        for c in range(nh // wc):
            dve.wait_ge(w_hi, c + 1)
            dst = slice(c * wc, (c + 1) * wc)
            dve.tensor_tensor(W.lo[:, dst, :], raw[c], f32(W.hi[:, dst, :]), ALU.subtract).then_inc(w_ready, 1)
            if c == 0:
                dve.wait_ge(a_hi, 1)
                dve.tensor_tensor(AS[0].lo[:], A[0], f32(AS[0].hi[:]), ALU.subtract).then_inc(a_lo, 1)
        tiles(dve, step)
        turned(NT - 1, 1)

    @block.tensor
    def _(pe):
        def turn(tt, j):
            pe.wait_ge(h3_made, tt + 1)
            wait(pe, h3_lo, tt - 1)
            for k in range(KC):
                last = pe.transpose(psH[j][:, k * P:(k + 1) * P], HN[j][:, k * P:(k + 1) * P], ident[:])
            last.then_inc(h3_turned, 1)

        def step(tt, j, i, more):
            pe.wait_ge(a_lo, tt + 1)
            wait(pe, x2_made, tt - 1)
            for h in range(nh):
                if h % wc == 0:
                    pe.wait_ge(w_ready, h // wc + 1)
                last = mm3(pe, psX[j][:], AS[j].at(ALL, h, ALL), W.at(ALL, h, ALL), h == 0, h == nh - 1)
            last.then_inc(proj, 1)
            if not (isinstance(tt, int) and tt == 0):
                turn(tt - 1, 1 - j)

        tiles(pe, step)
        turn(NT - 1, 1)


def build_experts(nc, ctx, sem, t, keep):
    acc, h3T, ident = keep["acc"], keep["h3T"], keep["ident"]
    w_gu = 2 * KC * I
    w_cols = w_gu + NIT * D
    ne = NE + 1

    def sb(name, shape, dt=F32):
        return ctx.enter_context(nc.sbuf_tensor(name, shape, dt))

    raw, w_in, gate_in = keep["w_ahead"], keep["wexp_in"], keep["gate_in"]
    W = [Pair(ctx, nc, f"wexp{j}", [P, w_cols]) for j in range(2)]
    Hd = Pair(ctx, nc, "hidden", [P, NIT, T])
    SG = [sb(f"silu{j}", [P, BANK]) for j in range(2)]
    HF = [sb(f"hidden_f32_{j}", [P, BANK]) for j in range(2)]
    gate_f, gate = keep["gate_f"], Pair(ctx, nc, "gate_w", [P, KC, NE])
    bias, tri, tri_g = sb("bias_rows", [P, NE]), sb("tri_rows", [P, NE, NE]), sb("tri_g_rows", [P, GS, GS])
    sig, V, wts = sb("scores", [P, NT, NE]), sb("biased", [P, NT, NE]), sb("weights", [P, NT, NE])
    rank, masked = sb("rank", [P, NT, NE]), sb("masked", [P, NT, NE])
    above, equal = sb("above", [P, NT, NE, NE]), sb("equal", [P, NT, NE, NE])
    gsum, grank, gmask, gpen = (sb(n, [P, NT, NG]) for n in ("gsum", "grank", "gmask", "gpen"))
    wsum = sb("wsum", [P, NT])
    cw = sb("expert_weight", [P, ne, NT])
    logits_t = sb("logits_t", [NE, T])

    psA = [ctx.enter_context(nc.psum_tensor(f"psA{j}", [P, 2, BANK], F32)) for j in range(2)]
    psD = [ctx.enter_context(nc.psum_tensor(f"psD{j}", [P, BANK], F32)) for j in range(4)]
    logits = psD[2][:, 0:NT * NE].rearrange("p (t e) -> p t e", e=NE)

    w_hi, w_lo, w0_lo = sem("wexp_hi"), sem("wexp_lo"), sem("wexp0_lo")
    route_in, gate_hi, gate_lo, logit_mm, logit_out, logit_turned, sig_made = (
        sem(n) for n in ("route_in", "gate_hi", "gate_lo", "logit_mm", "logit_out", "logit_turned", "sig_made"))
    route, ones_made, cw_made = sem("route"), sem("ones_made"), sem("cw_made")
    a_mm, silu_made, prod_made, hid_hi, hid_lo = (
        sem(n) for n in ("a_mm", "silu_made", "prod_made", "hid_hi", "hid_lo"))
    d_mm, acc_made, out_sem = sem("d_mm"), sem("acc_made"), sem("out_done")

    def experts(eng, step):
        for j in range(2):
            step(j, j, 0, True)
        with eng.Fori(1, ne // 2) as i:
            for j in range(2):
                step(2 * i + j, j, i, True)
        step(ne - 1, 0, ne // 2, False)

    M = 2 * NIT

    block = ctx.enter_context(nc.Block())

    @block.sync
    def _(sp):
        sp.dma_start(bias[:], t["bias"].to_broadcast([P, NE])).then_inc(route_in, 16)
        sp.dma_start(tri[:].rearrange("p i j -> p (i j)"), t["tri"].to_broadcast([P, NE * NE])).then_inc(route_in, 16)
        sp.dma_start(tri_g[:].rearrange("p i j -> p (i j)"), t["tri_g"].to_broadcast([P, GS * GS])).then_inc(route_in, 16)

        def load(e, j):
            sp.wait_ge(w_lo, e - 1)
            sp.dma_start(raw[j], t["w_exp"][e]).then_inc(w_in[j], 16)

        with sp.Fori(1, ne // 2) as i:
            for j in range(2):
                load(2 * i + j, j)
        load(ne - 1, 0)
        for tt in range(NT):
            sp.wait_ge(acc_made, NT * (ne - 1) + tt + 1)
            sp.dma_start(t["out"][tt], acc[:, tt, :]).then_inc(out_sem, 16)
        sp.wait_ge(out_sem, 16 * NT)

    @block.gpsimd
    def _(pool):
        def split(e, j):
            pool.wait_ge(w_hi, e + 1)
            pool.tensor_tensor(W[j].lo[:], raw[j], f32(W[j].hi[:]), ALU.subtract).then_inc(w_lo, 1)

        pool.memset(cw[:, 0, :], 1.0).then_inc(ones_made, 1)
        pool.wait_ge(w_hi, 1)
        pool.tensor_tensor(W[0].lo[:, w_gu:], raw[0][:, w_gu:], f32(W[0].hi[:, w_gu:]), ALU.subtract).then_inc(w0_lo, 1)
        pool.wait_ge(w0_lo, 2)
        pool.sem_inc(w_lo, 1)

        def step(e, j, i, more):
            if more:
                split(e + 1, 1 - j)
            for m in range(M):
                it, cols = m % NIT, slice(m // NIT * BANK, (m // NIT + 1) * BANK)
                pool.wait_ge(hid_hi, M * e + m + 1)
                pool.tensor_tensor(Hd.lo[:, it, cols], HF[m % 2][:], f32(Hd.hi[:, it, cols]),
                                   ALU.subtract).then_inc(hid_lo, 1)

        experts(pool, step)

    @block.scalar
    def _(act):
        def split(e, j, n):
            act.wait_ge(w_in[j], 16 * n)
            wait(act, d_mm, NT * (e - 1))
            act.copy(W[j].hi[:], raw[j]).then_inc(w_hi, 1)

        act.wait_ge(gate_in, 16)
        act.copy(gate.hi[:], gate_f[:]).then_inc(gate_hi, 1)
        split(0, 0, 1)
        for half in range(2):
            act.wait_ge(logit_mm, half + 1)
            act.copy(logits_t[:, half * BANK:(half + 1) * BANK], psD[half][0:NE, :]).then_inc(logit_out, 1)

        def step(e, j, i, more):
            if more:
                split(e + 1, 1 - j, i + 1 + j)
            for m in range(M):
                act.wait_ge(a_mm, M * e + m + 1)
                wait(act, prod_made, M * e + m - 1)
                act.activation(SG[m % 2][:], psA[m % 2][:, 0, :], ACT.Silu).then_inc(silu_made, 1)
                if isinstance(e, int) and e == 0 and m == 0:
                    act.wait_ge(logit_turned, 1)
                    act.activation(sig[:], logits, ACT.Sigmoid).then_inc(sig_made, 1)
                act.wait_ge(prod_made, M * e + m + 1)
                wait(act, d_mm, NT * e)
                cols = slice(m // NIT * BANK, (m // NIT + 1) * BANK)
                act.copy(Hd.hi[:, m % NIT, cols], HF[m % 2][:]).then_inc(hid_hi, 1)

        experts(act, step)

    @block.vector
    def _(dve):
        route_count = [0]

        def link(ins):
            route_count[0] += 1
            ins.then_inc(route, 1)
            dve.wait_ge(route, route_count[0])

        def ranks(values, n, size, tri_m, ab, eq, out):
            vj = values.unsqueeze(2).to_broadcast([P, n, size, size])
            vi = values.unsqueeze(3).to_broadcast([P, n, size, size])
            low = tri_m.unsqueeze(1).to_broadcast([P, n, size, size])
            dve.tensor_tensor(ab, vj, vi, ALU.is_gt).then_inc(route, 1)
            route_count[0] += 1
            link(dve.tensor_tensor(eq, vj, vi, ALU.is_equal))
            link(dve.tensor_tensor(eq, eq, low, ALU.mult))
            link(dve.tensor_tensor(ab, ab, eq, ALU.add))
            link(dve.tensor_reduce(out, ab, AX.X, ALU.add))

        def by_group(ap):
            return ap.rearrange("p t (g x) -> p (t g) x", x=GS)

        def small(ap, n, size):
            return ap[:].rearrange("p t i j -> p (t i j)")[:, 0:n * size * size].rearrange(
                "p (n i j) -> p n i j", i=size, j=size)

        def route_groups():
            dve.wait_ge(sig_made, 1)
            dve.wait_ge(route_in, 48)
            link(dve.tensor_tensor(V[:], sig[:], bias[:].unsqueeze(1).to_broadcast([P, NT, NE]), ALU.add))
            ranks(by_group(V[:]), NT * NG, GS, tri_g[:], small(above, NT * NG, GS), small(equal, NT * NG, GS),
                  by_group(rank[:]))
            link(dve.scalar_tensor_tensor(masked[:], rank[:], 2.0, V[:], ALU.is_lt, ALU.mult))
            link(dve.tensor_reduce(gsum[:].rearrange("p t g -> p (t g)"), by_group(masked[:]), AX.X, ALU.add))
            ranks(gsum[:], NT, NG, tri_g[:], small(above, NT, NG), small(equal, NT, NG), grank[:])
            link(dve.tensor_scalar(gmask[:], grank[:], float(TOPG), None, ALU.is_lt))
            link(dve.tensor_scalar(gpen[:], gmask[:], 1.0, 1e30, ALU.subtract, ALU.mult))

        def route_mask():
            wide = lambda ap: ap[:].rearrange("p t g -> p (t g)").unsqueeze(2).to_broadcast([P, NT * NG, GS])
            link(dve.tensor_tensor(by_group(masked[:]), by_group(V[:]), wide(gmask), ALU.mult))
            link(dve.tensor_tensor(by_group(masked[:]), by_group(masked[:]), wide(gpen), ALU.add))

        def route_experts():
            ranks(masked[:], NT, NE, tri[:], above[:], equal[:], rank[:])

        def route_weights():
            link(dve.scalar_tensor_tensor(wts[:], rank[:], float(TOPK), sig[:], ALU.is_lt, ALU.mult))
            link(dve.tensor_reduce(wsum[:], wts[:], AX.X, ALU.add))
            link(dve.tensor_scalar(wsum[:], wsum[:], 1e-20, None, ALU.add))
            link(dve.reciprocal(wsum[:], wsum[:]))
            link(dve.tensor_tensor(wts[:], wts[:], wsum[:].unsqueeze(2).to_broadcast([P, NT, NE]), ALU.mult))
            dve.tensor_scalar(cw[:, 1:, :].rearrange("p e t -> p t e"), wts[:], SCALING, None,
                              ALU.mult).then_inc(cw_made, 1)

        dve.wait_ge(gate_hi, 1)
        dve.tensor_tensor(gate.lo[:], gate_f[:], f32(gate.hi[:]), ALU.subtract).then_inc(gate_lo, 1)
        dve.wait_ge(w_hi, 1)
        dve.tensor_tensor(W[0].lo[:, 0:w_gu], raw[0][:, 0:w_gu], f32(W[0].hi[:, 0:w_gu]), ALU.subtract).then_inc(w0_lo, 1)

        def step(e, j, i, more):
            first = isinstance(e, int) and e == 0
            for m in range(M):
                dve.wait_ge(silu_made, M * e + m + 1)
                wait(dve, hid_lo, M * e + m - 1)
                dve.tensor_tensor(HF[m % 2][:], psA[m % 2][:, 1, :], SG[m % 2][:], ALU.mult).then_inc(prod_made, 1)
                if first and m < 2:
                    (route_groups, route_mask)[m]()
                if isinstance(e, int) and e == 1 and m < 2:
                    (route_experts, route_weights)[m]()
            if first:
                dve.wait_ge(ones_made, 1)
            elif isinstance(e, int) and e == 1:
                dve.wait_ge(cw_made, 1)
            for tt in range(NT):
                dve.wait_ge(d_mm, NT * e + tt + 1)
                wait(dve, acc_made, NT * e - NT + tt + 1)
                dve.scalar_tensor_tensor(acc[:, tt, :], psD[tt % 4][:],
                                         cw[:, bass.ds(e, 1), tt:tt + 1].rearrange("p o t -> p (o t)"),
                                         acc[:, tt, :], ALU.mult, ALU.add).then_inc(acc_made, 1)

        experts(dve, step)

    @block.tensor
    def _(pe):
        pe.wait_ge(gate_lo, 1)
        for half in range(2):
            for k in range(KC):
                last = mm3(pe, psD[half][0:NE, :], gate.at(ALL, k, ALL),
                           h3T.at(ALL, k, slice(half * BANK, (half + 1) * BANK)), k == 0, k == KC - 1)
            last.then_inc(logit_mm, 1)

        def turn_logits():
            pe.wait_ge(logit_out, 2)
            for tt in range(NT):
                last = pe.transpose(logits[:, tt, :], logits_t[:, tt * P:(tt + 1) * P], ident[0:NE, 0:NE])
            last.then_inc(logit_turned, 1)

        def step(e, j, i, more):
            if isinstance(e, int) and e == 0:
                pe.wait_ge(w0_lo, 2)
            else:
                pe.wait_ge(w_lo, e + 1)
            w = W[j]
            for m in range(M):
                it, cols = m % NIT, slice(m // NIT * BANK, (m // NIT + 1) * BANK)
                wait(pe, prod_made, M * e + m - 1)
                for a in range(2):
                    for k in range(KC):
                        at = (a * KC + k) * I + it * P
                        last = mm3(pe, psA[m % 2][:, a, :], w.at(ALL, slice(at, at + P)), h3T.at(ALL, k, cols),
                                   k == 0, k == KC - 1)
                last.then_inc(a_mm, 1)
                if isinstance(e, int) and e == 0 and m == 0:
                    turn_logits()
            for tt in range(NT):
                if tt % (NT // 2) == 0:
                    pe.wait_ge(hid_lo, M * e + (tt // (NT // 2) + 1) * NIT)
                wait(pe, acc_made, NT * e + tt - 3)
                if isinstance(e, int) and e == 0 and tt == 0:
                    pe.wait_ge(sig_made, 1)
                for k in range(NIT):
                    last = mm3(pe, psD[tt % 4][:], Hd.at(ALL, k, slice(tt * P, (tt + 1) * P)),
                               w.at(ALL, slice(w_gu + k * D, w_gu + (k + 1) * D)), k == 0, k == NIT - 1)
                last.then_inc(d_mm, 1)

        experts(pe, step)



def build(nc, t):
    outer = ExitStack()
    with outer:
        made = []

        def sem(name):
            made.append(name)
            return outer.enter_context(nc.semaphore(name))

        ident = outer.enter_context(nc.sbuf_tensor("ident", [P, P], F32))
        eps_pow = outer.enter_context(nc.sbuf_tensor("eps_pow", [P, 1], F32))
        keep = {"ident": ident, "eps_pow": eps_pow}
        early = outer.enter_context(nc.sbuf_tensor("early", [P, 4, LT * DC], F32))
        keep["early"] = [early[:, 2 * j:2 * j + 2].rearrange("p a (k c) -> p (a k) c", c=BANK) for j in range(2)]
        keep["kv_raw"], keep["kv_rope"], keep["kv_term"] = early[:, 0], early[:, 2], early[:, 3]
        keep["rope_tab"] = early[:, 1].rearrange("p (a x) -> p a x", a=2)
        for name in ("tab_in", "kv_in", "rope_part", "rope_done", "gate_in"):
            keep[name] = sem(name)
        for name, n in (("wqkv_in", HQ // REP + 1), ("wo_in", W_AHEAD), ("a_in", 2), ("wexp_in", 2)):
            keep[name] = [sem(f"{name}{j}") for j in range(n)]
        with ExitStack() as attn:
            keep["F"] = Pair(attn, nc, "F", [P, H, D])
            with ExitStack() as ctx:
                keep["h1T"] = Pair(ctx, nc, "h1T", [P, KC, T])
                build_queries(nc, ctx, sem, t, keep)
            with ExitStack() as ctx:
                build_cross(nc, ctx, sem, t, keep)
        ahead = outer.enter_context(nc.sbuf_tensor("w_ahead", [P, W_AHEAD, KC, BANK], F32))
        w_exp = 2 * KC * I + NIT * D
        flat = ahead[:].rearrange("p c k x -> p (c k x)")
        keep["ahead"] = [ahead[:, c] for c in range(W_AHEAD)]
        keep["w_ahead"] = [flat[:, j * w_exp:(j + 1) * w_exp] for j in range(2)]
        keep["gate_f"] = outer.enter_context(nc.sbuf_tensor("gate_f", [P, KC, NE], F32))
        with ExitStack() as ctx:
            build_self(nc, ctx, sem, t, keep)
        with ExitStack() as rest:
            keep["acc"] = rest.enter_context(nc.sbuf_tensor("acc", [P, NT, D], F32))
            keep["h3T"] = Pair(rest, nc, "h3T", [P, KC, T])
            with ExitStack() as ctx:
                build_project(nc, ctx, sem, t, keep)
            with ExitStack() as ctx:
                build_experts(nc, ctx, sem, t, keep)


def _pack_pairs(w_kc_q, W_qr, Wq, W_kr, w_kc_kv, Wo):
    kq = w_kc_q.reshape(NP, 2, P, QT, P).transpose(0, 4, 1, 3, 2).reshape(NP, P, W_KQ)
    qr = W_qr.reshape(NP, 2, QT, P, R).transpose(0, 3, 1, 2, 4).reshape(NP, P, W_QR)
    wq = Wq.reshape(NP, 2, P, D).transpose(0, 2, 1, 3).reshape(NP, P, W_Q)
    kr = W_kr.transpose(0, 2, 1).reshape(NP, P, P)
    kv = w_kc_kv.reshape(NP, 2, P, DC).transpose(0, 2, 1, 3).reshape(NP, P, W_KV)
    wo = Wo.T.reshape(NP, 2, P, D).transpose(0, 2, 1, 3).reshape(NP, P, W_O)
    return np.concatenate([kq, qr, wq, kr, kv, wo], axis=2)


def _rope_cross():
    inv = (1.0 / 10000.0 ** (np.arange(0, DC, 2, dtype=np.float32) / np.float32(DC))).astype(np.float32)
    freqs = (np.arange(L, dtype=np.float32)[:, None] * inv[None, :]).astype(np.float32)
    sign = np.where(np.arange(DC // 2) < DC // 4, -1.0, 1.0).astype(np.float32)
    return np.stack([np.cos(freqs), np.sin(freqs) * sign], 1).reshape(P, LT, 2, DC // 2).transpose(0, 2, 1, 3)


def _rope_self():
    inv = (1.0 / 10000.0 ** (np.arange(0, DH, 2, dtype=np.float32) / np.float32(DH))).astype(np.float32)
    ang = ((np.arange(P) % S).astype(np.float32)[:, None] * inv[None, :]).astype(np.float32)
    k = np.stack([np.cos(ang), -np.sin(ang), np.sin(ang)], 1)
    return np.stack([k * np.float32(DH ** -0.5), k], 1).astype(np.float32)


def _mask_self():
    m = np.where(np.arange(S)[None, :] <= np.arange(P)[:, None] % S, 0.0, -1e30).astype(np.float32)
    return np.tile(m, (1, BANK // S))


def _rows(w):
    return w.T.reshape(w.shape[1] // P, P, w.shape[0]).transpose(1, 0, 2)


def kernel(x, ctx_512, L0_xattn_Wq, L0_xattn_w_kc_q, L0_xattn_w_kc_kv, L0_xattn_W_qr, L0_xattn_W_kr,
           L0_xattn_Wo, L0_attn_w_qkv, L0_attn_w_o, L0_ffn_gate_weight, L0_ffn_expert_bias,
           L0_ffn_gate_proj, L0_ffn_up_proj, L0_ffn_down_proj, L0_ffn_shared_gate, L0_ffn_shared_up,
           L0_ffn_shared_down):
    import concourse.bacc as bacc
    from concourse.bass_utils import run_bass_kernel_spmd as run

    A = np.asarray
    w_qkv = A(L0_attn_w_qkv)
    nq = HQ * DH
    wkv_first = np.concatenate([w_qkv[nq:], w_qkv[:nq]], axis=0)
    gates = np.concatenate([A(L0_ffn_shared_gate)[None], A(L0_ffn_gate_proj)])
    ups = np.concatenate([A(L0_ffn_shared_up)[None], A(L0_ffn_up_proj)])
    downs = np.concatenate([A(L0_ffn_shared_down)[None], A(L0_ffn_down_proj)])
    gu = np.stack([gates, ups], 1).reshape(NE + 1, 2, I, KC, P).transpose(0, 4, 1, 3, 2)
    dn = downs.reshape(NE + 1, D, NIT, P).transpose(0, 3, 2, 1)
    arrays = {
        "x": A(x).reshape(NT, P, D),
        "ctx": A(ctx_512).reshape(B, P, LT * DC),
        "w_pairs": _pack_pairs(A(L0_xattn_w_kc_q), A(L0_xattn_W_qr), A(L0_xattn_Wq), A(L0_xattn_W_kr),
                               A(L0_xattn_w_kc_kv), A(L0_xattn_Wo)),
        "rope_x": _rope_cross().reshape(P, 2, LT * DC // 2),
        "w_qkv": _rows(wkv_first).reshape(P, KC, 5, BANK).transpose(2, 0, 1, 3),
        "rope_s": _rope_self(),
        "mask": _mask_self(),
        "w_o": _rows(A(L0_attn_w_o)),
        "gate_w": _rows(A(L0_ffn_gate_weight)),
        "bias": A(L0_ffn_expert_bias).reshape(1, NE),
        "tri": (np.arange(NE)[None, :] < np.arange(NE)[:, None]).astype(np.float32).reshape(1, NE * NE),
        "tri_g": (np.arange(GS)[None, :] < np.arange(GS)[:, None]).astype(np.float32).reshape(1, GS * GS),
        "w_exp": np.concatenate([gu.reshape(NE + 1, P, 2 * KC * I), dn.reshape(NE + 1, P, NIT * D)], 2),
    }
    arrays = {n: np.ascontiguousarray(a) for n, a in arrays.items()}
    nc = bacc.Bacc("TRN2", target_bir_lowering=False, num_devices=1)
    t = {n: nc.dram_tensor(n, a.shape, F32, kind="ExternalInput").ap() for n, a in arrays.items()}
    t["out"] = nc.dram_tensor("out", (NT, P, D), F32, kind="ExternalOutput").ap()
    t["qe"] = nc.dram_tensor("qe", (2, B, P, NP, 2 * S), F32).ap()
    t["x1"] = nc.dram_tensor("x1", (NT, P, D), F32).ap()
    t["h2T"] = nc.dram_tensor("h2T", (NT, P, 2, D), F32).ap()
    t["ao"] = nc.dram_tensor("ao", (NT, P, HQ // 2, P), F32).ap()
    build(nc, t)
    r = run(nc, [arrays], core_ids=[0])
    return r.results[0]["out"].reshape(B, S, D)
```
